# Optimizing a Trainium2 kernel written in Bass

```python
import numpy as np
import jax
import jax.numpy as jnp

def _softmax(x, axis=-1):
    return jax.nn.softmax(x, axis=axis)

def _gelu(x):
    return jax.nn.gelu(x, approximate=True)

def _silu(x):
    return jax.nn.silu(x)

def _sigmoid(x):
    return jax.nn.sigmoid(x)

def _layernorm(x, axis=-1, eps=1e-05):
    m = jnp.mean(x, axis=axis, keepdims=True)
    v = jnp.var(x, axis=axis, keepdims=True)
    return (x - m) / jnp.sqrt(v + eps)

def _scatter_add(tgt, idx, src, axis=0):
    return tgt.at[idx].add(src)

def _segment_sum(src, seg, n):
    return jax.ops.segment_sum(src, seg, n)
kernel_name = 'mk_adj_resnorm_d4_adj_r2_6814b6'

def setup_inputs(seed: int=0):
    np.random.seed(seed)
    _w = jnp.asarray

    def _rec_inputs():
        import jax
        import jax.numpy as jnp
        _gk = jax.random.key(seed)
        x = -0.0002928 + 1 * jax.random.normal(jax.random.fold_in(_gk, 1), (16, 512, 256), jnp.float32)
        _a = jax.random.bernoulli(jax.random.fold_in(_gk, 2), 0.03125, (512, 512))
        adj = _a.astype(jnp.int32)
        return (x, adj)
    x, adj = _rec_inputs()

    def _L0_gnn_setup():
        import jax, jax.numpy as jnp
        import numpy as np
        D_MODEL = 256
        NUM_HEADS = 8
        D_HEAD = D_MODEL // NUM_HEADS
        B, N = (4, 1024)
        key = jax.random.key(seed)
        ks = jax.random.split(key, 10)
        s = 1.0 / np.sqrt(D_MODEL)
        inp = {'h': jax.random.normal(ks[0], (B, N, D_MODEL), dtype=jnp.float32), 'adj': jax.random.randint(ks[1], (N, N), 0, 2, dtype=jnp.int32), 'Wq': jax.random.uniform(ks[2], (D_MODEL, D_MODEL), jnp.float32, -s, s), 'bq': jax.random.uniform(ks[3], (D_MODEL,), jnp.float32, -s, s), 'Wk': jax.random.uniform(ks[4], (D_MODEL, D_MODEL), jnp.float32, -s, s), 'bk': jax.random.uniform(ks[5], (D_MODEL,), jnp.float32, -s, s), 'Wv': jax.random.uniform(ks[6], (D_MODEL, D_MODEL), jnp.float32, -s, s), 'bv': jax.random.uniform(ks[7], (D_MODEL,), jnp.float32, -s, s), 'Wo': jax.random.uniform(ks[8], (D_MODEL, D_MODEL), jnp.float32, -s, s), 'bo': jax.random.uniform(ks[9], (D_MODEL,), jnp.float32, -s, s)}
        return inp
    _L0_gnn_all = _L0_gnn_setup()
    _L0_gnn_in = {k: v for k, v in _L0_gnn_all.items() if k in ('Wq', 'bq', 'Wk', 'bk', 'Wv', 'bv', 'Wo', 'bo')}
    del _L0_gnn_all

    def _L1_gnn_setup():
        import jax, jax.numpy as jnp
        import numpy as np
        B, K, DIN, DOUT = (32, 64, 256, 256)
        key = jax.random.key(seed)
        k1, k2, k3, k4 = jax.random.split(key, 4)
        x = jax.random.normal(k1, (B, K, DIN), dtype=jnp.float32)
        adj = jax.random.randint(k2, (K, K), 0, 2, dtype=jnp.int32)
        W = jax.random.normal(k3, (DOUT, 2 * DIN), dtype=jnp.float32) * 0.02
        b = jax.random.normal(k4, (DOUT,), dtype=jnp.float32) * 0.02
        return {'x': x, 'adj': adj, 'W': W, 'b': b}
    _L1_gnn_all = _L1_gnn_setup()
    _L1_gnn_in = {k: v for k, v in _L1_gnn_all.items() if k in ('W', 'b')}
    del _L1_gnn_all

    def _L2_gnn_setup():
        import jax, jax.numpy as jnp
        import numpy as np
        B, N, D = (8, 1024, 256)
        NEG_SLOPE = 0.2
        key = jax.random.key(seed)
        k1, k2, k3, k4, k5 = jax.random.split(key, 5)
        x = jax.random.normal(k1, (B, N, D), dtype=jnp.float32)
        adj = jax.random.randint(k2, (N, N), 0, 2, dtype=jnp.int32)
        adj = jnp.maximum(adj, jnp.eye(N, dtype=jnp.int32))
        W = jax.random.normal(k3, (D, D), dtype=jnp.float32) * (1.0 / np.sqrt(D))
        a_src = jax.random.normal(k4, (D,), dtype=jnp.float32) * (1.0 / np.sqrt(D))
        a_dst = jax.random.normal(k5, (D,), dtype=jnp.float32) * (1.0 / np.sqrt(D))
        return {'x': x, 'adj': adj, 'W': W, 'a_src': a_src, 'a_dst': a_dst}
    _L2_gnn_all = _L2_gnn_setup()
    _L2_gnn_in = {k: v for k, v in _L2_gnn_all.items() if k in ('W', 'a_src', 'a_dst')}
    del _L2_gnn_all

    def _L3_gnn_setup():
        import jax, jax.numpy as jnp
        import numpy as np
        B, K, DIN, DOUT = (32, 64, 256, 256)
        key = jax.random.key(seed)
        k1, k2, k3, k4 = jax.random.split(key, 4)
        x = jax.random.normal(k1, (B, K, DIN), dtype=jnp.float32)
        adj = jax.random.randint(k2, (K, K), 0, 2, dtype=jnp.int32)
        W = jax.random.normal(k3, (DOUT, 2 * DIN), dtype=jnp.float32) * 0.02
        b = jax.random.normal(k4, (DOUT,), dtype=jnp.float32) * 0.02
        return {'x': x, 'adj': adj, 'W': W, 'b': b}
    _L3_gnn_all = _L3_gnn_setup()
    _L3_gnn_in = {k: v for k, v in _L3_gnn_all.items() if k in ('W', 'b')}
    del _L3_gnn_all
    return {'x': x, 'adj': adj, 'L0_gnn_Wq': _L0_gnn_in['Wq'], 'L0_gnn_bq': _L0_gnn_in['bq'], 'L0_gnn_Wk': _L0_gnn_in['Wk'], 'L0_gnn_bk': _L0_gnn_in['bk'], 'L0_gnn_Wv': _L0_gnn_in['Wv'], 'L0_gnn_bv': _L0_gnn_in['bv'], 'L0_gnn_Wo': _L0_gnn_in['Wo'], 'L0_gnn_bo': _L0_gnn_in['bo'], 'L1_gnn_W': _L1_gnn_in['W'], 'L1_gnn_b': _L1_gnn_in['b'], 'L2_gnn_W': _L2_gnn_in['W'], 'L2_gnn_a_src': _L2_gnn_in['a_src'], 'L2_gnn_a_dst': _L2_gnn_in['a_dst'], 'L3_gnn_W': _L3_gnn_in['W'], 'L3_gnn_b': _L3_gnn_in['b']}

def reference(x, adj, L0_gnn_Wq, L0_gnn_bq, L0_gnn_Wk, L0_gnn_bk, L0_gnn_Wv, L0_gnn_bv, L0_gnn_Wo, L0_gnn_bo, L1_gnn_W, L1_gnn_b, L2_gnn_W, L2_gnn_a_src, L2_gnn_a_dst, L3_gnn_W, L3_gnn_b):
    import jax
    import jax.numpy as jnp

    def _L0_gnn_ref(h, adj, Wq, bq, Wk, bk, Wv, bv, Wo, bo):
        import jax, jax.numpy as jnp
        import numpy as np
        D_MODEL = 256
        NUM_HEADS = 8
        D_HEAD = D_MODEL // NUM_HEADS
        B, N = (4, 1024)
        b, n, _ = h.shape

        def split_heads(x):
            return x.reshape(b, n, NUM_HEADS, D_HEAD).transpose(0, 2, 1, 3)
        q = split_heads(h @ Wq.T + bq)
        k = split_heads(h @ Wk.T + bk)
        v = split_heads(h @ Wv.T + bv)
        scale = 1.0 / np.sqrt(D_HEAD)
        scores = jnp.einsum('bhqd,bhkd->bhqk', q, k) * scale
        mask = (adj == 0)[None, None, :, :]
        scores = jnp.where(mask, -jnp.inf, scores)
        attn = jax.nn.softmax(scores, axis=-1)
        out = jnp.einsum('bhqk,bhkd->bhqd', attn, v)
        out = out.transpose(0, 2, 1, 3).reshape(b, n, D_MODEL)
        return out @ Wo.T + bo

    def _L1_gnn_ref(x, adj, W, b):
        import jax, jax.numpy as jnp
        import numpy as np
        B, K, DIN, DOUT = (32, 64, 256, 256)
        Din = x.shape[-1]
        Wi, Wj = (W[:, :Din], W[:, Din:])
        mi = jnp.einsum('bkd,od->bko', x, Wi)
        mj = jnp.einsum('bkd,od->bko', x, Wj)
        a = adj.astype(x.dtype)
        deg = a.sum(axis=1)
        out = deg[None, :, None] * (mi + b) + jnp.einsum('ij,bjo->bio', a, mj)
        return out

    def _L2_gnn_ref(x, adj, W, a_src, a_dst):
        import jax, jax.numpy as jnp
        import numpy as np
        B, N, D = (8, 1024, 256)
        NEG_SLOPE = 0.2
        Wh = jnp.einsum('bnd,de->bne', x, W)
        e_src = jnp.einsum('bnd,d->bn', Wh, a_src)
        e_dst = jnp.einsum('bnd,d->bn', Wh, a_dst)
        logits = e_src[:, :, None] + e_dst[:, None, :]
        logits = jnp.where(logits >= 0, logits, NEG_SLOPE * logits)
        mask = (adj == 0)[None, :, :]
        logits = jnp.where(mask, -jnp.inf, logits)
        attn = jax.nn.softmax(logits, axis=-1)
        attn = jnp.nan_to_num(attn, nan=0.0)
        out = jnp.einsum('bnm,bmd->bnd', attn, Wh)
        return out

    def _L3_gnn_ref(x, adj, W, b):
        import jax, jax.numpy as jnp
        import numpy as np
        B, K, DIN, DOUT = (32, 64, 256, 256)
        Din = x.shape[-1]
        Wi, Wj = (W[:, :Din], W[:, Din:])
        mi = jnp.einsum('bkd,od->bko', x, Wi)
        mj = jnp.einsum('bkd,od->bko', x, Wj)
        a = adj.astype(x.dtype)
        deg = a.sum(axis=1)
        out = deg[None, :, None] * (mi + b) + jnp.einsum('ij,bjo->bio', a, mj)
        return out
    x = _layernorm(x + _L0_gnn_ref(x, adj, L0_gnn_Wq, L0_gnn_bq, L0_gnn_Wk, L0_gnn_bk, L0_gnn_Wv, L0_gnn_bv, L0_gnn_Wo, L0_gnn_bo), axis=-1)
    x = _layernorm(x + _L1_gnn_ref(x, adj, L1_gnn_W, L1_gnn_b), axis=-1)
    x = _layernorm(x + _L2_gnn_ref(x, adj, L2_gnn_W, L2_gnn_a_src, L2_gnn_a_dst), axis=-1)
    x = _layernorm(x + _L3_gnn_ref(x, adj, L3_gnn_W, L3_gnn_b), axis=-1)
    return x

_drawn_inputs = setup_inputs


def setup_inputs(seed=0):
    import zlib

    import numpy as np

    out = dict(_drawn_inputs(seed))
    spreads = {}
    factors = {'L0_gnn_bq': 27.168, 'L0_gnn_bk': 64.0}
    for name, (base, spread) in spreads.items():
        noise = np.random.default_rng([zlib.crc32(name.encode()), seed]).standard_normal(out[name].shape)
        drawn = base * np.exp(spread * noise) if base else spread * noise
        out[name] = jnp.asarray(drawn.astype(out[name].dtype))
    for name, factor in factors.items():
        out[name] = (out[name] * factor).astype(out[name].dtype)
    return out
```

```python
from contextlib import ExitStack

import concourse.bass as bass
from concourse import mybir

F32 = mybir.dt.float32
F16 = mybir.dt.float16
BF16 = mybir.dt.bfloat16
I32 = mybir.dt.int32
ALU = mybir.AluOpType
ACT = mybir.ActivationFunctionType
AX = mybir.AxisListType

P = 128
SLOTS = 32
XS = 16.0
WS = 1024.0
AXS = 4.0
EPS = 1e-5
SLOPE = 0.2
FAR = -3.0e38
LAYERS = (0, 1, 2, 3)

SIDE = [
    ("q", 0, 22), ("k", 0, 23), ("q", 1, 24), ("k", 1, 30),
    ("v", 0, 40), ("v", 1, 41),
    ("r", 0, 54), ("r", 1, 70),
    ("y0", 0, 73), ("y0", 1, 74),
    ("t1", 0, 78), ("t1", 1, 79), ("ax1", 0, 80), ("ax1", 1, 81),
    ("mi1", 0, 82), ("mi1", 1, 83), ("mj1", 0, 84), ("mj1", 1, 85),
    ("t2", 0, 89), ("t2", 1, 89), ("db", 0, 90), ("s", 0, 91), ("wh", 0, 92), ("wh", 1, 93),
    ("ta", 0, 96), ("ta", 1, 97), ("ta", 2, 98), ("ta", 3, 99), ("yo", 0, 99), ("yo", 1, 101),
    ("t3", 0, 106), ("t3", 1, 107), ("ax3", 0, 108), ("ax3", 1, 109),
    ("mi3", 0, 110), ("mi3", 1, 111), ("mj3", 0, 112), ("mj3", 1, 113),
]
SIDE_BANKS = 3
SIDE_ORDER = sorted(SIDE, key=lambda x: (x[2] % SLOTS, -x[2]))
PLACE = {(n, k): i for i, (n, k, _) in enumerate(SIDE_ORDER)}
SLOT_OF = {(n, k): s for n, k, s in SIDE}


def build(nc, x, xT, adj, adjT, wts, w_gat, a_src, a_dst, biases, out):
    B, N, D = x.shape
    H = 8
    DH = D // H
    NT = N // P
    NC = D // P
    UNITS = H * NT
    GROUP = 8
    LAST = 3
    assert (NT, NC, DH, UNITS) == (4, 2, 32, SLOTS)
    SCORE = 1.0 / DH ** 0.5 / (XS * XS)
    HALF = N // 2
    RING = 4
    assert UNITS % RING == 0

    with ExitStack() as ctx:
        def sb(name, shape, dt):
            return ctx.enter_context(nc.sbuf_tensor(name, shape, dt))

        def sem(name):
            return ctx.enter_context(nc.semaphore(name))

        NW = len(wts)
        w_hi = sb("w_hi", [P, NW, NC, D], F16)
        w_lo = sb("w_lo", [P, NW, NC, D], F16)
        names = ["q", "k", "v", "o", "1i", "1j", "2", "3i", "3j"]
        WH = {n: w_hi[:, i] for i, n in enumerate(names)}
        WL = {n: w_lo[:, i] for i, n in enumerate(names)}
        mask = sb("mask", [P, NT, N], BF16)
        aT = sb("aT", [P, NT, N], F16)
        deg = sb("deg", [P, NT], F32)
        deg_s = sb("deg_s", [P, NT], F32)
        ident = sb("ident", [P, P], F32)
        ident16 = sb("ident16", [P, P], F16)
        ones = sb("ones", [P, P], F32)
        NB = len(biases)
        bias_hl = sb("bias_hl", [P, NB, D], F16)
        BI = {n: bias_hl[:, i, :] for i, n in enumerate(["q", "k", "v", "o", "1", "3"])}
        ones_hl = sb("ones_hl", [P, N], F16)
        wa = sb("wa", [P, 2, NC], F32)
        wab = sb("wab", [P, 2, NC, P], F32)
        wab_h = sb("wab_h", [P, 2, NC, P], F16)
        wab_l = sb("wab_l", [P, 2, NC, P], F16)
        half_neg = sb("half_neg", [P, NT], F32)
        edges = sb("edges", [P, 2, NT], F32)
        power0 = sb("power0", [P, NT], F32)

        xt = sb("xt", [P, NC, N], F32)
        xt_h = sb("xt_h", [P, NC, N], F16)
        xt_l = sb("xt_l", [P, NC, N], F16)
        xr = sb("xr", [P, NT, D], F32)
        qk_h = sb("qk_h", [P, 4, N], F16)
        qk_l = sb("qk_l", [P, 4, N], F16)
        qp = sb("qp", [3 * DH, H, N], F16)
        kp = sb("kp", [3 * DH, H, N], F16)
        v = sb("v", [P, NT, D], F32)
        z = sb("z", [P, RING, N], F32)
        nmax = sb("nmax", [P, UNITS], F32)
        p = sb("p", [P, RING, N], F32)
        sum_p = sb("sum_p", [P, UNITS], F32)
        rinv = sb("rinv", [P, NT, 4, DH], F32)
        pT = sb("pT", [P, 2, 4, NT, HALF], F32)
        r_sb = sb("r_sb", [P, N], F32)
        o16 = sb("o16", [P, N], F32)
        o_h = sb("o_h", [P, NC, N], F16)
        o_l = sb("o_l", [P, NC, N], F16)
        res = {L: sb(f"res{L}", [P, NT, D], F32) for L in (1, 2, 3)}
        stats = sb("stats", [P, 4, NT, 6], F32)
        mv = sb("mv", [P, 4, NT, 2], F32)
        ve = sb("ve", [P, 4, NT], F32)
        rstd = sb("rstd", [P, 4, NT], F32)
        h_ = {L: sb(f"x{L}_h", [P, NT, D], F16) for L in (1, 3)}
        l_ = {L: sb(f"x{L}_l", [P, NT, D], F16) for L in (1, 3)}
        t_ = {L: sb(f"x{L}T", [P, 2, NC, N], F16) for L in (1, 2, 3)}
        ax = {L: sb(f"ax{L}", [P, 2, NC, N], F16) for L in (1, 3)}
        wh = sb("wh", [P, NT, D], F32)
        zm = sb("zm", [P, NT, N], F32)
        zs = sb("zs", [P, 2, N], F32)
        dmax = sb("dmax", [P, NT], F32)
        scol = sb("scol", [P, NT], F32)
        mcol = sb("mcol", [P, 2, NT], F32)
        nm2 = sb("nm2", [P, NT], F32)
        e = sb("e", [P, 2, N], F32)
        esum = sb("esum", [P, NT], F32)
        esum2 = sb("esum2", [P, NT], F32)
        einv = sb("einv", [P, NT], F32)
        eT = sb("eT", [P, NT, N], F32)

        bias32 = p[:, 0:NB * D // N, :].rearrange("p a (b d) -> p (a b) d", d=D)
        ab = v[:, 0:2, :]
        wg = v[:, 2:4, :]
        stage_w = pT[:].rearrange("p a g k q -> p (a g k q)")[:, 0:NW * NC * D].rearrange(
            "p (w c d) -> p w c d", w=NW, c=NC)
        stage_adj = zm[:].bitcast(I32)
        stage_adjT = eT[:].bitcast(I32)
        edge = z[:]

        s_ps = [ctx.enter_context(nc.psum_tensor(f"s_ps{i}", [P, N], F32)) for i in range(2)]
        pt_ps = [ctx.enter_context(nc.psum_tensor(f"pt_ps{i}", [P, N], F32)) for i in range(2)]
        o_ps = ctx.enter_context(nc.psum_tensor("o_ps", [P, N], F32))
        side_ps = [ctx.enter_context(nc.psum_tensor(f"side_ps{i}", [P, N], F32)) for i in range(SIDE_BANKS)]

        consts_loaded = sem("consts_loaded")
        setup_pool = sem("setup_pool")
        setup_act = sem("setup_act")
        setup_dve = sem("setup_dve")
        wab_ready = sem("wab_ready")
        empty_step, power0_ready = sem("empty_step"), sem("power0_ready")
        xt_loaded, xr_loaded, stored = sem("xt_loaded"), sem("xr_loaded"), sem("stored")
        xt_scaled, xt_hi, xt_lo, xr_scaled = sem("xt_scaled"), sem("xt_hi"), sem("xt_lo"), sem("xr_scaled")
        qk_done, qk_hi, qk_lo = sem("qk_done"), sem("qk_hi"), sem("qk_lo")
        packed = [sem(f"packed{i}") for i in range(4)]
        v_done, v_ready = sem("v_done"), sem("v_ready")
        s_done, z_ready, p_ready, pt_done, pt_ready = (
            sem("s_done"), sem("z_ready"), sem("p_ready"), sem("pt_done"), sem("pt_ready"))
        pv_done, rinv_ready, r_done, r_ready, o_ready, o_hi, o_lo = (
            sem("pv_done"), sem("rinv_ready"), sem("r_done"), sem("r_ready"), sem("o_ready"), sem("o_hi"),
            sem("o_lo"))
        y0_done, y0_ready = sem("y0_done"), sem("y0_ready")
        st_ready = [sem(f"st_ready{L}") for L in LAYERS]
        mv_ready = [sem(f"mv_ready{L}") for L in LAYERS]
        ve_ready = [sem(f"ve_ready{L}") for L in LAYERS]
        rstd_ready = [sem(f"rstd_ready{L}") for L in LAYERS]
        ln_ready = [sem(f"ln_ready{L}") for L in LAYERS]
        two = lambda name: {L: sem(f"{name}{L}") for L in (1, 3)}
        x_hi, x_lo, xT_done, xT_ready = two("x_hi"), two("x_lo"), two("xT_done"), two("xT_ready")
        ax_done, ax_hi, ax_lo = two("ax_done"), two("ax_hi"), two("ax_lo")
        mi_done, mi_ready, mj_done, mj_ready = two("mi_done"), two("mi_ready"), two("mj_done"), two("mj_ready")
        t2_done, t2_hi, t2_lo = sem("t2_done"), sem("t2_hi"), sem("t2_lo")
        db_done, zm_ready, s_col_done, scol_ready, wh_done, wh_ready = (
            sem("db_done"), sem("zm_ready"), sem("s_col_done"), sem("scol_ready"), sem("wh_done"), sem("wh_ready"))
        m_step, nm2_ready, zs_ready, lz_ready, e_ready, einv_step, einv_ready = (
            sem("m_step"), sem("nm2_ready"), sem("zs_ready"), sem("lz_ready"), sem("e_ready"), sem("einv_step"),
            sem("einv_ready"))
        ta_done, eT_ready, yo_done, y2_ready = sem("ta_done"), sem("eT_ready"), sem("yo_done"), sem("y2_ready")

        def count(per, b, k=0):
            value = per * b + k
            return max(0, value) if isinstance(value, int) else value

        def early(eng, value):
            if not isinstance(value, int):
                eng.compute_val(value)
            return value

        bank_read = {
            "q": (qk_lo, 4, lambda k: 2 * k + 1), "k": (qk_lo, 4, lambda k: 2 * k + 2),
            "v": (v_ready, 2, lambda k: k + 1), "r": (r_ready, 2, lambda k: k + 1),
            "y0": (y0_ready, 2, lambda k: k + 1),
            "t2": (t2_lo, 2, lambda k: k + 1), "db": (zm_ready, NT, lambda k: NT), "s": (scol_ready, 1, lambda k: 1),
            "wh": (wh_ready, 2, lambda k: k + 1), "ta": (eT_ready, NT, lambda k: k + 1),
            "yo": (y2_ready, NT, lambda k: 2 * k + 2),
        }
        for L in (1, 3):
            bank_read[f"t{L}"] = (xT_ready[L], 2, lambda k: k + 1)
            bank_read[f"ax{L}"] = (ax_lo[L], 2, lambda k: k + 1)
            bank_read[f"mi{L}"] = (mi_ready[L], NT, lambda k: 2 * k + 2)
            bank_read[f"mj{L}"] = (mj_ready[L], 2, lambda k: k + 1)

        def side_bank(name, part):
            return side_ps[PLACE[name, part] % SIDE_BANKS]

        def bank_free(name, part, b):
            me = PLACE[name, part]
            step, place = b + SLOT_OF[name, part] // SLOTS, me
            for _ in range(3 * len(SIDE)):
                place -= SIDE_BANKS
                if place < 0:
                    step, place = step - 1, place + len(SIDE) // SIDE_BANKS * SIDE_BANKS + (
                        SIDE_BANKS if me % SIDE_BANKS < len(SIDE) % SIDE_BANKS else 0)
                n, k, slot = SIDE_ORDER[place]
                if alive(step - slot // SLOTS):
                    s, per, read = bank_read[n]
                    return s, count(per, step - slot // SLOTS, read(k))
            return setup_act, 0

        def alive(b):
            return not isinstance(b, int) or 0 <= b < B

        def run_steps(eng, step):
            for j in range(LAST + 1):
                step(j)
            with eng.Fori(LAST + 1, B) as j:
                step(j)
            for j in range(B, B + LAST + 1):
                step(j)

        def unit(u):
            grp, r = divmod(u, GROUP)
            return 2 * (grp % 2) + r % 2, r // 2, grp // 2, grp % 2

        def sum_column(u):
            t, g, c, _ = unit(u)
            return (c * NT + t) * 4 + g

        def due(slot, table):
            return [(part, s // SLOTS) for part, s in table if s % SLOTS == slot]

        block = ctx.enter_context(nc.Block())

        @block.sync
        def _(sp):
            for i, w in enumerate(wts):
                sp.dma_start(stage_w[:, i], w.rearrange("(c p) o -> p c o", p=P)).then_inc(consts_loaded, 16)
            sp.dma_start(wg, w_gat.rearrange("(c p) o -> p c o", p=P)).then_inc(consts_loaded, 16)
            sp.dma_start(stage_adj, adj.rearrange("(t p) j -> p t j", p=P)).then_inc(consts_loaded, 16)
            sp.dma_start(stage_adjT, adjT.rearrange("(t p) j -> p t j", p=P)).then_inc(consts_loaded, 16)
            sp.wait_ge(setup_pool, 1)
            for i, b in enumerate(biases):
                for row in (0, 32):
                    sp.dma_start(bias32[row:row + 1, i, :], b.unsqueeze(0)).then_inc(consts_loaded, 16)
            for i, a in enumerate((a_src, a_dst)):
                sp.dma_start(ab[:, i, :], a.unsqueeze(0).broadcast_to([P, D])).then_inc(consts_loaded, 16)

            def load_xt(b):
                sp.wait_ge(xt_hi, count(1, b))
                sp.wait_ge(xt_lo, count(1, b))
                sp.dma_start(xt[:], xT[b].rearrange("(c p) n -> p c n", p=P)).then_inc(xt_loaded, 16)

            def load_xr(b):
                sp.wait_ge(y0_ready, count(2, b))
                sp.dma_start(xr[:], x[b].rearrange("(t p) d -> p t d", p=P)).then_inc(xr_loaded, 16)

            def pack(b, n):
                split = early(sp, count(4, b, n + 1))
                scored = early(sp, count(UNITS, b - 1, UNITS // 2 * (n // 2 + 1)))
                sp.wait_ge(setup_pool, 1)
                sp.wait_ge(qk_hi, split)
                sp.wait_ge(qk_lo, split)
                sp.wait_ge(s_done, scored)
                dst, parts = (qp, (qk_h, qk_l, qk_h)) if n % 2 == 0 else (kp, (qk_h, qk_h, qk_l))
                for g in range(4):
                    for r in range(3):
                        sp.dma_start(dst[DH * r:DH * r + DH, 4 * (n // 2) + g, :],
                                     parts[r][DH * g:DH * g + DH, n, :]).then_inc(packed[n], 16)

            def store(b):
                sp.wait_ge(ln_ready[3], count(NT, b + 1))
                sp.dma_start(out[b].rearrange("(t p) d -> p t d", p=P), res[3][:]).then_inc(stored, 16)

            def step(j):
                for slot in range(SLOTS):
                    for _, lag in due(slot, [(0, 16)]):
                        if alive(j - lag):
                            load_xt(j - lag)
                    for n, lag in due(slot, [(0, 24), (1, 25), (2, 31), (3, 31)]):
                        if alive(j - lag):
                            pack(j - lag, n)
                    for _, lag in due(slot, [(0, 44)]):
                        if alive(j - lag):
                            load_xr(j - lag)
                    for _, lag in due(slot, [(0, 117)]):
                        if alive(j - lag):
                            store(j - lag)

            run_steps(sp, step)
            sp.wait_ge(stored, 16 * B)

        @block.gpsimd
        def _(pool):
            pool.memset(p[:, 0:NB * D // N, :], 0.0).then_inc(setup_pool, 1)
            pool.memset(ident[:], 0.0).then_inc(setup_pool, 1)
            pool.memset(ident16[:], 0.0).then_inc(setup_pool, 1)
            pool.memset(ones[:], 1.0).then_inc(setup_pool, 1)
            pool.memset(ones_hl[:], XS).then_inc(setup_pool, 1)
            pool.memset(half_neg[:], -0.5).then_inc(setup_pool, 1)
            pool.memset(bias_hl[:], 0.0).then_inc(setup_pool, 1)
            pool.wait_ge(setup_pool, 7)
            for m in (ident, ident16):
                pool.affine_select(out=m[:], in_=m[:], compare_op=ALU.not_equal, fill=1.0, base=0,
                                   pattern=[[-1, P]], channel_multiplier=1).then_inc(setup_pool, 1)

            def scale_xt(b):
                loaded = early(pool, count(16, b + 1))
                pool.wait_ge(setup_pool, 1)
                pool.wait_ge(xt_loaded, loaded)
                pool.tensor_scalar(xt[:], xt[:], XS, 1.0, ALU.mult, ALU.mult).then_inc(xt_scaled, 1)

            def split_xt(b):
                pool.wait_ge(xt_hi, count(1, b + 1))
                pool.wait_ge(v_done, count(2, b))
                pool.tensor_tensor(xt_l[:], xt[:], xt_h[:], ALU.subtract).then_inc(xt_lo, 1)

            def scale_xr(b):
                loaded = early(pool, count(16, b + 1))
                pool.wait_ge(setup_pool, 1)
                pool.wait_ge(xr_loaded, loaded)
                pool.tensor_scalar(xr[:], xr[:], XS, 1.0, ALU.mult, ALU.mult).then_inc(xr_scaled, 1)

            def split_o(b, c):
                pool.wait_ge(o_hi, count(NC, b, c + 1))
                pool.wait_ge(y0_done, count(2, b))
                pool.tensor_tensor(o_l[:, c, :], o16[:], o_h[:, c, :], ALU.subtract).then_inc(o_lo, 1)

            def split_x(b, L):
                pool.wait_ge(x_hi[L], count(1, b + 1))
                pool.wait_ge(ax_done[L], count(NC, b))
                pool.tensor_tensor(l_[L][:], res[L][:], h_[L][:], ALU.subtract).then_inc(x_lo[L], 1)

            def rsqrt(b, L):
                c1, c2 = (1.0 / (XS * XS), EPS) if L < 3 else (1.0, EPS * XS * XS)
                variances = early(pool, count(NT, b + 1))
                pool.wait_ge(setup_pool, 1)
                pool.wait_ge(mv_ready[L], variances)
                pool.tensor_scalar(ve[:, L, :], mv[:, L, :, 1], c1, c2, ALU.mult, ALU.add).then_inc(ve_ready[L], 1)
                pool.wait_ge(ve_ready[L], count(1, b + 1))
                if L == 0:
                    pool.wait_ge(power0_ready, 1)
                pool.tensor_tensor(rstd[:, L, :], ve[:, L, :], (half_neg if L else power0)[:], ALU.pow).then_inc(rstd_ready[L], 1)

            def step(j):
                for slot in range(SLOTS):
                    for L, lag in due(slot, [(0, 75), (1, 87), (2, 103), (3, 115)]):
                        if alive(j - lag):
                            rsqrt(j - lag, L)
                    for c, lag in due(slot, [(0, 56), (1, 72)]):
                        if alive(j - lag):
                            split_o(j - lag, c)
                    for L, lag in due(slot, [(1, 77), (3, 105)]):
                        if alive(j - lag):
                            split_x(j - lag, L)
                    for _, lag in due(slot, [(0, 18)]):
                        if alive(j - lag):
                            scale_xt(j - lag)
                    for _, lag in due(slot, [(0, 19)]):
                        if alive(j - lag):
                            split_xt(j - lag)
                    for _, lag in due(slot, [(0, 49)]):
                        if alive(j - lag):
                            scale_xr(j - lag)

            run_steps(pool, step)

        @block.scalar
        def _(act):
            act.wait_ge(consts_loaded, 16 * (NW + 3 + 2 * NB + 2))
            act.activation(w_hi[:], stage_w, ACT.Copy, scale=WS).then_inc(setup_act, 1)
            act.wait_ge(setup_pool, 9)
            act.activation(bias_hl[0:1], bias32[0:1], ACT.Copy, scale=WS).then_inc(setup_act, 1)
            act.activation(bias_hl[32:33], bias32[32:33], ACT.Copy, scale=WS).then_inc(setup_act, 1)
            act.wait_ge(wab_ready, 1)
            act.activation(wab_h[:], wab[:], ACT.Copy, scale=WS).then_inc(setup_act, 1)

            def exp_scores(b, u):
                act.wait_ge(z_ready, count(UNITS, b, u + 1))
                act.wait_ge(pt_done, count(UNITS, b, u - RING + 1))
                act.wait_ge(rinv_ready, count(2, b - 1, u // 16 + 1))
                act.activation(p[:, u % RING, :], z[:, u % RING, :], ACT.Exp, bias=nmax[:, u:u + 1], scale=-1.0,
                               accum_out=sum_p[:, sum_column(u):sum_column(u) + 1]).then_inc(p_ready, 1)

            def evict_pt(b, u):
                t, g, _, _ = unit(u)
                grp = u // GROUP
                act.wait_ge(pt_done, count(UNITS, b, u + 1))
                act.wait_ge(pv_done, count(4, b, grp - 1))
                act.activation(pT[:, grp % 2, g, :, P * (t % 2):P * (t % 2) + P],
                               pt_ps[u % 2][:].rearrange("p (k q) -> p k q", k=NT), ACT.Copy).then_inc(pt_ready, 1)

            def xt_high(b):
                act.wait_ge(xt_scaled, count(1, b + 1))
                act.wait_ge(v_done, count(2, b))
                act.activation(xt_h[:], xt[:], ACT.Copy).then_inc(xt_hi, 1)

            def qk_high(b, n):
                act.wait_ge(qk_done, count(4, b, n + 1))
                act.wait_ge(packed[n], count(192, b))
                act.activation(qk_h[:, n, :], side_bank("qk"[n % 2], n // 2)[:], ACT.Copy,
                               scale=1.0 / WS).then_inc(qk_hi, 1)

            def v_evict(b, i):
                act.wait_ge(v_done, count(2, b, i + 1))
                act.wait_ge(pv_done, count(4, b))
                act.activation(v[:, 2 * i:2 * i + 2, :].rearrange("p t d -> p (t d)"), side_bank("v", i)[:],
                               ACT.Copy, scale=1.0 / (XS * WS)).then_inc(v_ready, 1)

            def r_evict(b, c):
                act.wait_ge(r_done, count(NC, b, c + 1))
                act.wait_ge(o_ready, count(NC, b, c))
                act.activation(r_sb[:], side_bank("r", c)[:], ACT.Copy, scale=XS).then_inc(r_ready, 1)

            def o_high(b, c):
                act.wait_ge(o_ready, count(NC, b, c + 1))
                act.wait_ge(y0_done, count(2, b))
                act.activation(o_h[:, c, :], o16[:], ACT.Copy).then_inc(o_hi, 1)

            def x_high(b, L):
                act.wait_ge(ln_ready[L - 1], count(NT, b + 1))
                act.wait_ge(ax_done[L], count(NC, b))
                act.activation(h_[L][:], res[L][:], ACT.Copy).then_inc(x_hi[L], 1)

            def ax_high(b, L, c):
                act.wait_ge(ax_done[L], count(NC, b, c + 1))
                act.wait_ge(mj_done[L], count(2, b))
                act.activation(ax[L][:, 0, c, :], side_bank(f"ax{L}", c)[:], ACT.Copy,
                               scale=AXS / XS).then_inc(ax_hi[L], 1)

            def t2_high(b, c):
                act.wait_ge(t2_done, count(NC, b, c + 1))
                act.wait_ge(wh_done, count(2, b))
                act.activation(t_[2][:, 0, c, :], side_bank("t2", c)[:], ACT.Copy).then_inc(t2_hi, 1)

            def wh_evict(b, i):
                act.wait_ge(wh_done, count(2, b, i + 1))
                act.wait_ge(yo_done, count(2, b))
                act.activation(wh[:, 2 * i:2 * i + 2, :].rearrange("p t d -> p (t d)"), side_bank("wh", i)[:],
                               ACT.Copy, scale=1.0 / (XS * WS)).then_inc(wh_ready, 1)

            def exp_gat(b, t):
                act.wait_ge(lz_ready, count(NT, b, t + 1))
                act.wait_ge(nm2_ready, count(1, b + 1))
                act.wait_ge(ta_done, count(NT, b, t - 1))
                act.wait_ge(einv_ready, count(1, b))
                act.activation(e[:, t % 2, :], zm[:, t, :], ACT.Exp, bias=nm2[:, t:t + 1], scale=1.0,
                               accum_out=esum[:, t:t + 1]).then_inc(e_ready, 1)

            def eT_evict(b, t):
                act.wait_ge(ta_done, count(NT, b, t + 1))
                act.wait_ge(yo_done, count(2, b))
                act.activation(eT[:, :, P * t:P * t + P],
                               side_bank("ta", t)[:].rearrange("p (k q) -> p k q", k=NT),
                               ACT.Copy).then_inc(eT_ready, 1)

            def step(j):
                for slot in range(SLOTS):
                    for u, lag in due(slot, [(u, 33 + u) for u in range(UNITS)]):
                        if alive(j - lag):
                            exp_scores(j - lag, u)
                    for u, lag in due(slot, [(u, 35 + u) for u in range(UNITS)]):
                        if alive(j - lag):
                            evict_pt(j - lag, u)
                    for L, lag in due(slot, [(3, 105), (1, 77)]):
                        if alive(j - lag):
                            x_high(j - lag, L)
                    for c, lag in due(slot, [(0, 108), (1, 109)]):
                        if alive(j - lag):
                            ax_high(j - lag, 3, c)
                    for t, lag in due(slot, [(t, 96 + t) for t in range(NT)]):
                        if alive(j - lag):
                            eT_evict(j - lag, t)
                    for t, lag in due(slot, [(t, 94 + t) for t in range(NT)]):
                        if alive(j - lag):
                            exp_gat(j - lag, t)
                    for i, lag in due(slot, [(0, 92), (1, 93)]):
                        if alive(j - lag):
                            wh_evict(j - lag, i)
                    for c, lag in due(slot, [(0, 89), (1, 89)]):
                        if alive(j - lag):
                            t2_high(j - lag, c)
                    for c, lag in due(slot, [(0, 80), (1, 81)]):
                        if alive(j - lag):
                            ax_high(j - lag, 1, c)
                    for c, lag in due(slot, [(0, 54), (1, 70)]):
                        if alive(j - lag):
                            r_evict(j - lag, c)
                    for c, lag in due(slot, [(0, 55), (1, 71)]):
                        if alive(j - lag):
                            o_high(j - lag, c)
                    for i, lag in due(slot, [(0, 40), (1, 41)]):
                        if alive(j - lag):
                            v_evict(j - lag, i)
                    for _, lag in due(slot, [(0, 18)]):
                        if alive(j - lag):
                            xt_high(j - lag)
                    for n, lag in due(slot, [(0, 22), (1, 23), (2, 24), (3, 30)]):
                        if alive(j - lag):
                            qk_high(j - lag, n)

            run_steps(act, step)

        @block.vector
        def _(dve):
            dve.wait_ge(consts_loaded, 16 * (NW + 3 + 2 * NB + 2))
            dve.tensor_scalar(mask[:], stage_adj, 0.0, FAR, ALU.is_equal, ALU.mult).then_inc(setup_dve, 1)
            dve.tensor_reduce(deg[:], stage_adj, AX.X, ALU.add).then_inc(setup_dve, 1)
            dve.tensor_copy(aT[:], stage_adjT).then_inc(setup_dve, 1)
            dve.tensor_scalar(edge, stage_adj, 0.0, None, ALU.not_equal).then_inc(setup_dve, 1)
            dve.wait_ge(setup_dve, 4)
            dve.tensor_scalar(deg_s[:], deg[:], 1.0 / WS, None, ALU.mult).then_inc(setup_dve, 1)
            dve.tensor_reduce(edges[:, 0, :], edge, AX.X, ALU.add).then_inc(empty_step, 1)
            dve.wait_ge(empty_step, 1)
            dve.reciprocal(edges[:, 1, :], edges[:, 0, :]).then_inc(empty_step, 1)
            dve.wait_ge(empty_step, 2)
            dve.tensor_scalar(power0[:], edges[:, 1, :], 0.0, -0.5, ALU.mult, ALU.add).then_inc(power0_ready, 1)
            for i in range(2):
                for c in range(NC):
                    dve.tensor_tensor_reduce(zs[:, 0, 0:D], wg[:, c, :], ab[:, i, :], 1.0, 0.0, ALU.mult, ALU.add,
                                             wa[:, i, c:c + 1]).then_inc(setup_dve, 1)
                    dve.wait_ge(setup_dve, 6 + 2 * i + c)
            dve.wait_ge(setup_pool, 9)
            for i in range(2):
                for c in range(NC):
                    wab_i = dve.tensor_scalar(wab[:, i, c, :], ones[:], wa[:, i, c:c + 1], None, ALU.mult)
            wab_i.then_inc(wab_ready, 1)
            dve.wait_ge(setup_act, 3)
            dve.scalar_tensor_tensor(w_lo[:].rearrange("p w c d -> p (w c d)"), stage_w.rearrange("p w c d -> p (w c d)"), WS,
                                     w_hi[:].rearrange("p w c d -> p (w c d)"),
                                     ALU.mult, ALU.subtract).then_inc(setup_dve, 1)
            dve.scalar_tensor_tensor(bias_hl[32:33], bias32[32:33], WS, bias_hl[32:33],
                                     ALU.mult, ALU.subtract).then_inc(setup_dve, 1)
            dve.wait_ge(setup_act, 4)
            dve.scalar_tensor_tensor(wab_l[:].rearrange("p a c q -> p (a c q)"),
                                     wab[:].rearrange("p a c q -> p (a c q)"), WS,
                                     wab_h[:].rearrange("p a c q -> p (a c q)"),
                                     ALU.mult, ALU.subtract).then_inc(setup_dve, 1)

            def row_max(b, u):
                t = unit(u)[0]
                scored, freed = early(dve, count(UNITS, b, u + 1)), early(dve, count(UNITS, b, u - RING + 1))
                dve.wait_ge(setup_pool, 1)
                dve.wait_ge(s_done, scored)
                dve.wait_ge(p_ready, freed)
                dve.tensor_tensor_reduce(z[:, u % RING, :], s_ps[u % 2][:], mask[:, t, :], -SCORE, -FAR,
                                         ALU.add, ALU.min, nmax[:, u:u + 1]).then_inc(z_ready, 1)

            def qk_low(b, n):
                dve.wait_ge(qk_hi, count(4, b, n + 1))
                dve.scalar_tensor_tensor(qk_l[:, n, :], side_bank("qk"[n % 2], n // 2)[:], 1.0 / WS, qk_h[:, n, :],
                                         ALU.mult, ALU.subtract).then_inc(qk_lo, 1)

            def sum_inverse(b, c):
                dve.wait_ge(p_ready, count(UNITS, b, UNITS // 2 * (c + 1)))
                dve.wait_ge(r_done, count(NC, b, c))
                dve.reciprocal(rinv[:].rearrange("p t g d -> p (t g) d"),
                               sum_p[:, 16 * c:16 * c + 16].unsqueeze(2).broadcast_to([P, 16, DH])
                               ).then_inc(rinv_ready, 1)

            def normalise(b, c):
                dve.wait_ge(r_ready, count(NC, b, c + 1))
                dve.wait_ge(pv_done, count(4, b, 2 * c + 2))
                dve.wait_ge(o_hi, count(NC, b, c))
                dve.wait_ge(o_lo, count(NC, b, c))
                dve.tensor_tensor(o16[:], o_ps[:], r_sb[:], ALU.mult).then_inc(o_ready, 1)

            def add_y0(b, i):
                dve.wait_ge(y0_done, count(2, b, i + 1))
                dve.wait_ge(xr_scaled, count(1, b + 1))
                if i == 0:
                    dve.wait_ge(x_hi[1], count(1, b))
                    dve.wait_ge(x_lo[1], count(1, b))
                dve.scalar_tensor_tensor(
                    res[1][:, 2 * i:2 * i + 2, :].rearrange("p t d -> p (t d)"), side_bank("y0", i)[:], 1.0 / WS,
                    xr[:, 2 * i:2 * i + 2, :].rearrange("p t d -> p (t d)"),
                    ALU.mult, ALU.add).then_inc(y0_ready, 1)

            def ln_stats(b, L, t, src):
                dve.bn_stats(stats[:, L, t, :], src[:, t, :]).then_inc(st_ready[L], 1)

            def ln_mean_var(b, L):
                for t in range(NT):
                    statistics = early(dve, count(NT, b, t + 1))
                    dve.wait_ge(setup_pool, 1)
                    dve.wait_ge(st_ready[L], statistics)
                    dve.bn_aggr(mv[:, L, t, :], stats[:, L, t, :]).then_inc(mv_ready[L], 1)

            def ln_apply(b, L, src, dst):
                dve.wait_ge(rstd_ready[L], count(1, b + 1))
                for t in range(NT):
                    dve.tensor_scalar(dst[:, t, :], src[:, t, :], mv[:, L, t, 0:1], rstd[:, L, t:t + 1],
                                      ALU.subtract, ALU.mult).then_inc(ln_ready[L], 1)

            def xT_evict(b, L, w):
                dve.wait_ge(xT_done[L], count(2, b, w + 1))
                dve.wait_ge(mi_done[L], count(2, b))
                dve.tensor_copy(t_[L][:, w].rearrange("p c n -> p (c n)"),
                                side_bank(f"t{L}", w)[:].bitcast(F16)).then_inc(xT_ready[L], 1)

            def ax_low(b, L, c):
                dve.wait_ge(ax_hi[L], count(NC, b, c + 1))
                dve.scalar_tensor_tensor(ax[L][:, 1, c, :], side_bank(f"ax{L}", c)[:], AXS / XS, ax[L][:, 0, c, :],
                                         ALU.mult, ALU.subtract).then_inc(ax_lo[L], 1)

            def add_mi(b, L, i):
                dve.wait_ge(mi_done[L], count(2, b, i + 1))
                for t in (2 * i, 2 * i + 1):
                    dve.scalar_tensor_tensor(res[L][:, t, :], side_bank(f"mi{L}", i)[:, D * (t % 2):D * (t % 2) + D],
                                             deg_s[:, t:t + 1], res[L][:, t, :],
                                             ALU.mult, ALU.add).then_inc(mi_ready[L], 1)

            def add_mj(b, L, i):
                dve.wait_ge(mj_done[L], count(2, b, i + 1))
                dve.wait_ge(mi_ready[L], count(NT, b, 2 * i + 2))
                pair = res[L][:, 2 * i:2 * i + 2, :].rearrange("p t d -> p (t d)")
                dve.scalar_tensor_tensor(pair, side_bank(f"mj{L}", i)[:], XS / (AXS * WS), pair,
                                         ALU.mult, ALU.add).then_inc(mj_ready[L], 1)

            def stats_after(b, L, i, s):
                dve.wait_ge(s, count(2, b, i + 1))
                for t in (2 * i, 2 * i + 1):
                    ln_stats(b, L, t, res[L])

            def t2_low(b, c):
                dve.wait_ge(t2_hi, count(NC, b, c + 1))
                dve.tensor_tensor(t_[2][:, 1, c, :], side_bank("t2", c)[:], t_[2][:, 0, c, :],
                                  ALU.subtract).then_inc(t2_lo, 1)

            def neighbour_max(b):
                done, freed = early(dve, count(1, b + 1)), early(dve, count(NT, b))
                dve.wait_ge(setup_pool, 1)
                dve.wait_ge(db_done, done)
                dve.wait_ge(e_ready, freed)
                for t in range(NT):
                    dve.tensor_tensor_reduce(zm[:, t, :], side_bank("db", 0)[:], mask[:, t, :], 1.0 / (XS * WS),
                                             FAR, ALU.add, ALU.max, dmax[:, t:t + 1]).then_inc(zm_ready, 1)

            def logit_max(b):
                dve.wait_ge(s_col_done, count(1, b + 1))
                dve.tensor_scalar(scol[:], side_bank("s", 0)[:, 0:NT], 1.0 / (XS * WS), None,
                                  ALU.mult).then_inc(scol_ready, 1)
                dve.wait_ge(scol_ready, count(1, b + 1))
                dve.wait_ge(zm_ready, count(NT, b + 1))
                dve.tensor_tensor(mcol[:, 0, :], dmax[:], scol[:], ALU.add).then_inc(m_step, 1)
                dve.wait_ge(m_step, count(2, b, 1))
                dve.scalar_tensor_tensor(mcol[:, 1, :], mcol[:, 0, :], SLOPE, mcol[:, 0, :],
                                         ALU.mult, ALU.max).then_inc(m_step, 1)
                dve.wait_ge(m_step, count(2, b, 2))
                dve.tensor_scalar(nm2[:], mcol[:, 1, :], -1.0e30, -1.0, ALU.max, ALU.mult).then_inc(nm2_ready, 1)

            def logits(b, t):
                dve.wait_ge(lz_ready, count(NT, b, t - 1))
                dve.tensor_scalar(zs[:, t % 2, :], zm[:, t, :], scol[:, t:t + 1], SLOPE,
                                  ALU.add, ALU.mult).then_inc(zs_ready, 1)
                dve.wait_ge(zs_ready, count(NT, b, t + 1))
                dve.scalar_tensor_tensor(zm[:, t, :], zm[:, t, :], scol[:, t:t + 1], zs[:, t % 2, :],
                                         ALU.add, ALU.max).then_inc(lz_ready, 1)

            def gat_inverse(b):
                dve.wait_ge(e_ready, count(NT, b + 1))
                dve.tensor_scalar(esum2[:], esum[:], 1.0e-30, 1.0 / XS, ALU.max, ALU.mult).then_inc(einv_step, 1)
                dve.wait_ge(einv_step, count(1, b + 1))
                dve.reciprocal(einv[:], esum2[:]).then_inc(einv_ready, 1)

            def add_yo(b, i):
                dve.wait_ge(yo_done, count(2, b, i + 1))
                dve.wait_ge(einv_ready, count(1, b + 1))
                for t in (2 * i, 2 * i + 1):
                    dve.scalar_tensor_tensor(res[2][:, t, :], side_bank("yo", i)[:, D * (t % 2):D * (t % 2) + D],
                                             einv[:, t:t + 1], res[2][:, t, :],
                                             ALU.mult, ALU.add).then_inc(y2_ready, 1)

            def stats_yo(b, i):
                dve.wait_ge(y2_ready, count(NT, b, 2 * i + 2))
                for t in (2 * i, 2 * i + 1):
                    ln_stats(b, 2, t, res[2])

            def step(j):
                for slot in range(SLOTS):
                    for u, lag in due(slot, [(u, 32 + u) for u in range(UNITS)]):
                        if alive(j - lag):
                            row_max(j - lag, u)
                    for w, lag in due(slot, [(0, 106), (1, 107)]):
                        if alive(j - lag):
                            xT_evict(j - lag, 3, w)
                    for c, lag in due(slot, [(0, 108), (1, 109)]):
                        if alive(j - lag):
                            ax_low(j - lag, 3, c)
                    for i, lag in due(slot, [(0, 110), (1, 111)]):
                        if alive(j - lag):
                            add_mi(j - lag, 3, i)
                    for i, lag in due(slot, [(0, 112), (1, 113)]):
                        if alive(j - lag):
                            add_mj(j - lag, 3, i)
                            stats_after(j - lag, 3, i, mj_ready[3])
                    for _, lag in due(slot, [(0, 114)]):
                        if alive(j - lag):
                            ln_mean_var(j - lag, 3)
                    for _, lag in due(slot, [(0, 116)]):
                        if alive(j - lag):
                            ln_apply(j - lag, 3, res[3], res[3])
                    for i, lag in due(slot, [(0, 100), (1, 102)]):
                        if alive(j - lag):
                            if i == 0:
                                gat_inverse(j - lag)
                            add_yo(j - lag, i)
                            stats_yo(j - lag, i)
                    for _, lag in due(slot, [(0, 102)]):
                        if alive(j - lag):
                            ln_mean_var(j - lag, 2)
                    for _, lag in due(slot, [(0, 104)]):
                        if alive(j - lag):
                            dve.wait_ge(stored, count(16, j - lag))
                            ln_apply(j - lag, 2, res[2], res[3])
                    for c, lag in due(slot, [(0, 89), (1, 89)]):
                        if alive(j - lag):
                            t2_low(j - lag, c)
                    for _, lag in due(slot, [(0, 91)]):
                        if alive(j - lag):
                            neighbour_max(j - lag)
                    for _, lag in due(slot, [(0, 92)]):
                        if alive(j - lag):
                            logit_max(j - lag)
                    for t, lag in due(slot, [(0, 93), (1, 93), (2, 94), (3, 95)]):
                        if alive(j - lag):
                            logits(j - lag, t)
                    for w, lag in due(slot, [(0, 78), (1, 79)]):
                        if alive(j - lag):
                            xT_evict(j - lag, 1, w)
                    for c, lag in due(slot, [(0, 80), (1, 81)]):
                        if alive(j - lag):
                            ax_low(j - lag, 1, c)
                    for i, lag in due(slot, [(0, 82), (1, 83)]):
                        if alive(j - lag):
                            add_mi(j - lag, 1, i)
                    for i, lag in due(slot, [(0, 84), (1, 85)]):
                        if alive(j - lag):
                            add_mj(j - lag, 1, i)
                            stats_after(j - lag, 1, i, mj_ready[1])
                    for _, lag in due(slot, [(0, 86)]):
                        if alive(j - lag):
                            ln_mean_var(j - lag, 1)
                    for _, lag in due(slot, [(0, 88)]):
                        if alive(j - lag):
                            ln_apply(j - lag, 1, res[1], res[2])
                    for i, lag in due(slot, [(0, 73), (1, 74)]):
                        if alive(j - lag):
                            add_y0(j - lag, i)
                            dve.wait_ge(y0_ready, count(2, j - lag, i + 1))
                            for t in (2 * i, 2 * i + 1):
                                ln_stats(j - lag, 0, t, res[1])
                    for _, lag in due(slot, [(0, 74)]):
                        if alive(j - lag):
                            ln_mean_var(j - lag, 0)
                    for _, lag in due(slot, [(0, 76)]):
                        if alive(j - lag):
                            ln_apply(j - lag, 0, res[1], res[1])
                    for c, lag in due(slot, [(0, 52), (1, 68)]):
                        if alive(j - lag):
                            sum_inverse(j - lag, c)
                    for c, lag in due(slot, [(0, 55), (1, 71)]):
                        if alive(j - lag):
                            normalise(j - lag, c)
                    for n, lag in due(slot, [(0, 22), (1, 23), (2, 24), (3, 30)]):
                        if alive(j - lag):
                            qk_low(j - lag, n)

            run_steps(dve, step)

        @block.tensor
        def _(pe):
            pe.wait_ge(setup_dve, 12)
            pe.wait_ge(setup_act, 4)

            def scores(b, u):
                t, g, c, _ = unit(u)
                h = 4 * c + g
                pe.wait_ge(packed[2 * c], count(192, b + 1))
                pe.wait_ge(packed[2 * c + 1], count(192, b + 1))
                pe.wait_ge(z_ready, count(UNITS, b, u - 1))
                pe.matmul(s_ps[u % 2][:], qp[:, h, P * t:P * t + P], kp[:, h, :],
                          start=True, stop=True).then_inc(s_done, 1)

            def transpose_p(b, u):
                pe.wait_ge(p_ready, count(UNITS, b, u + 1))
                pe.wait_ge(pt_ready, count(UNITS, b, u - 1))
                for k in range(NT):
                    mm = pe.transpose(pt_ps[u % 2][:, P * k:P * k + P], p[:, u % RING, P * k:P * k + P], ident[:])
                mm.then_inc(pt_done, 1)

            def times_v(b, grp, part):
                c, th = divmod(grp, 2)
                if part == 0:
                    pe.wait_ge(pt_ready, count(UNITS, b, GROUP * (grp + 1)))
                    pe.wait_ge(v_ready, count(2, b + 1))
                    if th == 0:
                        pe.wait_ge(o_ready, count(NC, b, c))
                for k in (2 * part, 2 * part + 1):
                    for g in range(4):
                        h = 4 * c + g
                        mm = pe.matmul(o_ps[DH * g:DH * g + DH, HALF * th:HALF * th + HALF],
                                       v[:, k, DH * h:DH * h + DH], pT[:, grp % 2, g, k, :],
                                       start=(k == 0), stop=(k == NT - 1))
                if part == 1:
                    mm.then_inc(pv_done, 1)

            def product(dst, pairs, bias=None):
                if bias is not None:
                    pe.matmul(dst, bias[0], bias[1], start=True, stop=False)
                for n, (lhs, rhs) in enumerate(pairs):
                    mm = pe.matmul(dst, lhs, rhs, start=(n == 0 and bias is None), stop=(n == len(pairs) - 1))
                return mm

            def split_pairs(lhs_h, lhs_l, rhs_h, rhs_l):
                return [(lhs_h, rhs_h), (lhs_l, rhs_h), (lhs_h, rhs_l)]

            def project_T(dst, w, c, xh, xl, bias):
                o = slice(P * c, P * c + P)
                pairs = [q for k in range(NC) for q in split_pairs(WH[w][:, k, o], WL[w][:, k, o],
                                                                   xh[:, k, :], xl[:, k, :])]
                return product(dst[:], pairs, (bias[:, o], ones_hl[:]))

            def project(dst, w, i, xh, xl, bias=None):
                for t in (2 * i, 2 * i + 1):
                    o = slice(P * t, P * t + P)
                    pairs = [q for k in range(NC) for q in split_pairs(xh[:, k, o], xl[:, k, o],
                                                                       WH[w][:, k, :], WL[w][:, k, :])]
                    mm = product(dst[:, D * (t % 2):D * (t % 2) + D], pairs,
                                 None if bias is None else (ones_hl[:, 0:P], bias))
                return mm

            def qk(b, n):
                pe.wait_ge(xt_hi, count(1, b + 1))
                pe.wait_ge(xt_lo, count(1, b + 1))
                w = "qk"[n % 2]
                pe.wait_ge(*bank_free(w, n // 2, b))
                bank = side_bank(w, n // 2)
                project_T(bank, w, n // 2, xt_h, xt_l, BI[w]).then_inc(qk_done, 1)

            def values(b, i):
                pe.wait_ge(*bank_free("v", i, b))
                bank = side_bank("v", i)
                project(bank, "v", i, xt_h, xt_l, BI["v"]).then_inc(v_done, 1)

            def spread_inverse(b, c):
                pe.wait_ge(rinv_ready, count(NC, b, c + 1))
                pe.wait_ge(*bank_free("r", c, b))
                bank = side_bank("r", c)
                for t in range(NT):
                    mm = pe.transpose(bank[:, P * t:P * t + P], rinv[:, t].rearrange("p g d -> p (g d)"), ident[:])
                mm.then_inc(r_done, 1)

            def output(b, i):
                pe.wait_ge(o_hi, count(NC, b + 1))
                pe.wait_ge(o_lo, count(NC, b + 1))
                pe.wait_ge(*bank_free("y0", i, b))
                bank = side_bank("y0", i)
                project(bank, "o", i, o_h, o_l, BI["o"]).then_inc(y0_done, 1)

            def transpose_x(b, L, w):
                pe.wait_ge((x_hi, x_lo)[w][L], count(1, b + 1))
                pe.wait_ge(*bank_free(f"t{L}", w, b))
                bank = side_bank(f"t{L}", w)[:].bitcast(F16)
                src = (h_, l_)[w][L]
                for c in range(NC):
                    for t in range(NT):
                        mm = pe.transpose(bank[:, N * c + P * t:N * c + P * t + P], src[:, t, P * c:P * c + P],
                                          ident16[:])
                mm.then_inc(xT_done[L], 1)

            def aggregate(b, L, c):
                pe.wait_ge(*bank_free(f"ax{L}", c, b))
                bank = side_bank(f"ax{L}", c)
                pairs = [(s[L][:, t, P * c:P * c + P], aT[:, t, :]) for s in (h_, l_) for t in range(NT)]
                product(bank[:], pairs).then_inc(ax_done[L], 1)

            def own_term(b, L, i):
                pe.wait_ge(xT_ready[L], count(2, b + 1))
                pe.wait_ge(*bank_free(f"mi{L}", i, b))
                bank = side_bank(f"mi{L}", i)
                project(bank, f"{L}i", i, t_[L][:, 0], t_[L][:, 1], BI[str(L)]).then_inc(mi_done[L], 1)

            def neighbour_term(b, L, i):
                pe.wait_ge(ax_lo[L], count(NC, b + 1))
                pe.wait_ge(*bank_free(f"mj{L}", i, b))
                bank = side_bank(f"mj{L}", i)
                project(bank, f"{L}j", i, ax[L][:, 0], ax[L][:, 1]).then_inc(mj_done[L], 1)

            def transpose_x2(b, c):
                pe.wait_ge(ln_ready[1], count(NT, b + 1))
                pe.wait_ge(*bank_free("t2", c, b))
                bank = side_bank("t2", c)
                for t in range(NT):
                    mm = pe.transpose(bank[:, P * t:P * t + P], res[2][:, t, P * c:P * c + P], ident[:])
                mm.then_inc(t2_done, 1)

            def gat_dst(b):
                pe.wait_ge(t2_lo, count(NC, b + 1))
                pe.wait_ge(*bank_free("db", 0, b))
                bank = side_bank("db", 0)
                pairs = [q for k in range(NC) for q in split_pairs(wab_h[:, 1, k, :], wab_l[:, 1, k, :],
                                                                   t_[2][:, 0, k, :], t_[2][:, 1, k, :])]
                product(bank[:], pairs).then_inc(db_done, 1)

            def gat_src(b):
                pe.wait_ge(*bank_free("s", 0, b))
                bank = side_bank("s", 0)
                for t in range(NT):
                    o = slice(P * t, P * t + P)
                    pairs = [q for k in range(NC) for q in split_pairs(t_[2][:, 0, k, o], t_[2][:, 1, k, o],
                                                                       wab_h[:, 0, k, 0:1], wab_l[:, 0, k, 0:1])]
                    mm = product(bank[:, t:t + 1], pairs)
                mm.then_inc(s_col_done, 1)

            def gat_wh(b, i):
                pe.wait_ge(*bank_free("wh", i, b))
                bank = side_bank("wh", i)
                project(bank, "2", i, t_[2][:, 0], t_[2][:, 1]).then_inc(wh_done, 1)

            def transpose_e(b, t):
                pe.wait_ge(e_ready, count(NT, b, t + 1))
                pe.wait_ge(*bank_free("ta", t, b))
                bank = side_bank("ta", t)
                for k in range(NT):
                    mm = pe.transpose(bank[:, P * k:P * k + P], e[:, t % 2, P * k:P * k + P], ident[:])
                mm.then_inc(ta_done, 1)

            def gat_out(b, i, t):
                pe.wait_ge(eT_ready, count(NT, b, t + 1))
                if t % 2 == 0:
                    pe.wait_ge(wh_ready, count(2, b + 1))
                    pe.wait_ge(*bank_free("yo", i, b))
                bank = side_bank("yo", i)
                mm = product(bank[:, D * (t % 2):D * (t % 2) + D],
                             [(eT[:, k, P * t:P * t + P], wh[:, k, :]) for k in range(NT)])
                if t % 2 == 1:
                    mm.then_inc(yo_done, 1)

            def step(j):
                for slot in range(SLOTS):
                    for u, lag in due(slot, [(u, 32 + u) for u in range(UNITS)]):
                        if alive(j - lag):
                            scores(j - lag, u)
                    for u, lag in due(slot, [(u, 35 + u) for u in range(UNITS)]):
                        if alive(j - lag):
                            transpose_p(j - lag, u)
                    for grp, lag in due(slot, [(grp, 44 + 8 * grp) for grp in range(4)]):
                        if alive(j - lag):
                            times_v(j - lag, grp, 0)
                    for grp, lag in due(slot, [(grp, 45 + 8 * grp) for grp in range(4)]):
                        if alive(j - lag):
                            times_v(j - lag, grp, 1)
                    for name, part, s in SIDE_ORDER:
                        b = j - s // SLOTS
                        if s % SLOTS != slot or not alive(b):
                            continue
                        if name in ("q", "k"):
                            qk(b, 2 * part + "qk".index(name))
                        elif name == "v":
                            values(b, part)
                        elif name == "r":
                            spread_inverse(b, part)
                        elif name == "y0":
                            output(b, part)
                        elif name == "t2":
                            transpose_x2(b, part)
                        elif name == "db":
                            gat_dst(b)
                        elif name == "s":
                            gat_src(b)
                        elif name == "wh":
                            gat_wh(b, part)
                        elif name == "ta":
                            transpose_e(b, part)
                        elif name == "yo":
                            gat_out(b, part, 2 * part)
                            gat_out(b, part, 2 * part + 1)
                        elif name[:-1] == "t":
                            transpose_x(b, int(name[-1]), part)
                        elif name[:-1] == "ax":
                            aggregate(b, int(name[-1]), part)
                        elif name[:-1] == "mi":
                            own_term(b, int(name[-1]), part)
                        elif name[:-1] == "mj":
                            neighbour_term(b, int(name[-1]), part)

            run_steps(pe, step)


def kernel(x, adj, L0_gnn_Wq, L0_gnn_bq, L0_gnn_Wk, L0_gnn_bk, L0_gnn_Wv, L0_gnn_bv, L0_gnn_Wo, L0_gnn_bo,
           L1_gnn_W, L1_gnn_b, L2_gnn_W, L2_gnn_a_src, L2_gnn_a_dst, L3_gnn_W, L3_gnn_b):
    import numpy as np
    import concourse.bacc as bacc
    from concourse.bass_utils import run_bass_kernel_spmd

    nc = bacc.Bacc("TRN2", target_bir_lowering=False, num_devices=1)
    arrays = {}

    def given(name, a):
        a = np.ascontiguousarray(a)
        arrays[name] = a
        return nc.dram_tensor(name, a.shape, mybir.dt.from_np(a.dtype), kind="ExternalInput").ap()

    D = x.shape[2]
    x, adj = np.asarray(x), np.asarray(adj)
    w1, w3 = np.asarray(L1_gnn_W), np.asarray(L3_gnn_W)
    weights = [("wq", np.asarray(L0_gnn_Wq).T), ("wk", np.asarray(L0_gnn_Wk).T), ("wv", np.asarray(L0_gnn_Wv).T),
               ("wo", np.asarray(L0_gnn_Wo).T), ("w1i", w1[:, :D].T), ("w1j", w1[:, D:].T),
               ("w2", np.asarray(L2_gnn_W)), ("w3i", w3[:, :D].T), ("w3j", w3[:, D:].T)]
    wts = [given(n, a) for n, a in weights]
    biases = [given(n, a) for n, a in (("bq", L0_gnn_bq), ("bk", L0_gnn_bk), ("bv", L0_gnn_bv), ("bo", L0_gnn_bo),
                                       ("b1", L1_gnn_b), ("b3", L3_gnn_b))]
    out = nc.dram_tensor("out", x.shape, F32, kind="ExternalOutput").ap()
    build(nc, given("x", x), given("xT", x.transpose(0, 2, 1)), given("adj", adj), given("adjT", adj.T), wts,
          wts[6], given("a_src", L2_gnn_a_src), given("a_dst", L2_gnn_a_dst), biases, out)
    r = run_bass_kernel_spmd(nc, [arrays], core_ids=[0])
    return r.results[0]["out"]
```

```python
from contextlib import ExitStack

import concourse.bass as bass
from concourse import mybir

F32 = mybir.dt.float32
F16 = mybir.dt.float16
BF16 = mybir.dt.bfloat16
I32 = mybir.dt.int32
ALU = mybir.AluOpType
ACT = mybir.ActivationFunctionType
AX = mybir.AxisListType

P = 128
SLOTS = 64
XS = 16.0
WS = 1024.0
ES = 1024.0
AXS = 4.0
EPS = 1e-5
SLOPE = 0.2
FAR = -3.0e38
LAYERS = (0, 1, 2, 3)

UNIT = range(0, SLOTS, 2)
SETUP_SLOTS = [2, 8, 16, 22, 28, 34, 40, 46, 52]
WHEN = {
    "sync": {"load_xt": [2], "pack": [26, 69], "load_xr": [92], "store": [250]},
    "gpsimd": {"scale_xt": [15], "split_xt": [19], "split_qk": [30, 32, 36, 39], "shift_xr": [102],
               "split_x1": [165], "add_bias1": [166], "split_x3": [224], "add_bias3": [229],
               "rsqrt": [164, 184, 216, 234]},
    "scalar": {"exp_scores": [68 + u for u in UNIT], "evict_pt": [72 + u for u in UNIT], "xt_high": [20],
               "qk_high": [26, 33, 41, 48], "v_evict": [80, 82], "r_evict": [104, 143], "o_high": [108, 153],
               "x_high1": [168], "ax_high1": [173, 177], "xT_high1": [170, 171], "xT_high2": [193, 193],
               "xT_high3": [228, 234], "exp_gat": [208, 208, 210, 210], "wh_high": [202, 204],
               "eT_high": [210, 210, 212, 215], "x_high3": [226], "ax_high3": [234, 234]},
    "vector": {"row_max": [64 + u for u in UNIT], "evict_qk": [24, 31, 39, 44], "sum_inverse": [99, 133],
               "normalise": [104, 149], "o_low": [111, 153], "add_y0": [156, 160], "mean_var0": [164],
               "apply0": [166, 166], "xT_low1": [170, 172], "ax_low1": [172, 177], "add_mi1": [177, 180],
               "add_mj1": [180, 185], "mean_var1": [185], "apply1": [189, 189], "xT_low2": [192, 193],
               "neighbour_max": [201, 201, 201, 201], "logit_max": [201], "logits": [205, 205, 209, 209],
               "wh_low": [204, 206], "eT_low": [210, 210, 210, 215], "add_yo": [216, 219], "mean_var2": [220],
               "apply2": [224, 224], "xT_low3": [229, 234], "ax_low3": [234, 234], "add_mi3": [234, 234],
               "add_mj3": [234, 234], "mean_var3": [244], "apply3": [254, 254]},
    "tensor": {"scores": [64 + u for u in UNIT], "transpose_p": [72 + u for u in UNIT],
               "times_v": [88, 100, 105, 106, 125, 126, 145, 145], "q": [24, 36], "k": [28, 44], "v": [81, 82],
               "r": [102, 142], "y0": [156, 161], "t1": [170, 170], "ax1": [172, 177], "mi1": [177, 180],
               "mj1": [181, 185], "t2": [193, 193], "db": [196], "s": [202], "wh": [202, 204],
               "ta": [210, 210, 212, 215], "yo": [215, 218], "t3": [228, 234], "ax3": [234, 234], "mi3": [234, 234],
               "mj3": [234, 234]},
}
SIDE_STAGES = ["q", "k", "v", "r", "y0", "t1", "ax1", "mi1", "mj1", "t2", "db", "s", "wh", "ta", "yo", "t3", "ax3",
               "mi3", "mj3"]
SIDE = [(name, part, slot) for name in SIDE_STAGES for part, slot in enumerate(WHEN["tensor"][name])]
SIDE_BANKS = 3
SIDE_ORDER = sorted(SIDE, key=lambda x: (x[2] % SLOTS, -x[2]))
PLACE = {(n, k): i for i, (n, k, _) in enumerate(SIDE_ORDER)}
SLOT_OF = {(n, k): s for n, k, s in SIDE}


def build(nc, x, xT, adj, adjT, wts, w_gat, a_src, a_dst, b_col_in, b_out, b_layer, out):
    B, N, D = x.shape
    H = 8
    DH = D // H
    NT = N // P
    NC = D // P
    UNITS = H * NT
    GROUP = 8
    LAST = 3
    assert (NT, NC, DH, 2 * UNITS) == (4, 2, 32, SLOTS)
    SCORE = 1.0 / DH ** 0.5 / (XS * XS)
    HALF = N // 2
    RING = 4
    assert UNITS % RING == 0

    with ExitStack() as ctx:
        def sb(name, shape, dt):
            return ctx.enter_context(nc.sbuf_tensor(name, shape, dt))

        def sem(name):
            return ctx.enter_context(nc.semaphore(name))

        NW = len(wts)
        w_hi = sb("w_hi", [P, NW, NC, D], F16)
        w_lo = sb("w_lo", [P, NW, NC, D], F16)
        names = ["q", "k", "v", "o", "1i", "1j", "2", "3i", "3j"]
        WH = {n: w_hi[:, i] for i, n in enumerate(names)}
        WL = {n: w_lo[:, i] for i, n in enumerate(names)}
        mask = sb("mask", [P, NT, N], BF16)
        aT = sb("aT", [P, NT, N], F16)
        deg = sb("deg", [P, NT], F32)
        deg_s = sb("deg_s", [P, NT], F32)
        ident = sb("ident", [P, P], F32)
        b_col = sb("b_col", [P, 3, NC], F32)
        bo_row = sb("bo_row", [P, D], F32)
        deg_b = {L: sb(f"deg_b{L}", [P, NT, D], F32) for L in (1, 3)}
        wa = sb("wa", [P, 2, NC], F32)
        wab_h = sb("wab_h", [P, 2, NC, P], F16)
        wab_l = sb("wab_l", [P, 2, NC, P], F16)
        half_neg = sb("half_neg", [P, NT], F32)
        edges = sb("edges", [P, 2, NT], F32)
        power0 = sb("power0", [P, NT], F32)

        xt = sb("xt", [P, NC, N], F32)
        xt_h = sb("xt_h", [P, NC, N], F16)
        xt_l = sb("xt_l", [P, NC, N], F16)
        xr = sb("xr", [P, NT, D], F32)
        qk = sb("qk", [P, 2, N], F32)
        qk16 = sb("qk16", [P, NC, 4, N], F16)
        HIGH, LOW = {"q": 1, "k": 2}, {"q": 0, "k": 3}
        qkp = sb("qkp", [3 * DH, 2, H, N], F16)
        v = sb("v", [P, NT, D], F32)
        z = sb("z", [P, RING, N], F32)
        nmax = sb("nmax", [P, UNITS], F32)
        p = sb("p", [P, RING, N], F32)
        sum_p = sb("sum_p", [P, UNITS], F32)
        rsum = sb("rsum", [P, NC, 16], F32)
        rinv = sb("rinv", [P, NT, 4, DH], F32)
        pT = sb("pT", [P, 2, 4, NT, HALF], F32)
        o16 = sb("o16", [P, N], F32)
        o_h = sb("o_h", [P, NC, N], F16)
        o_l = sb("o_l", [P, NC, N], F16)
        res = {L: sb(f"res{L}", [P, NT, D], F32) for L in (1, 2, 3)}
        stats = sb("stats", [P, 4, NT, 6], F32)
        mv = sb("mv", [P, 4, NT, 2], F32)
        ve = sb("ve", [P, 4, NT], F32)
        rstd = sb("rstd", [P, 4, NT], F32)
        h_ = {L: sb(f"x{L}_h", [P, NT, D], F16) for L in (1, 3)}
        l_ = {L: sb(f"x{L}_l", [P, NT, D], F16) for L in (1, 3)}
        t_ = {L: sb(f"x{L}T", [P, 2, NC, N], F16) for L in (1, 2, 3)}
        ax = {L: sb(f"ax{L}", [P, 2, NC, N], F16) for L in (1, 3)}
        wh = sb("wh", [P, 2, NT, D], F16)
        zm = sb("zm", [P, NT, N], F32)
        zs = sb("zs", [P, 2, N], F32)
        dmax = sb("dmax", [P, NT], F32)
        scol = sb("scol", [P, NT], F32)
        mcol = sb("mcol", [P, 2, NT], F32)
        nm2 = sb("nm2", [P, NT], F32)
        e = sb("e", [P, 2, N], F32)
        esum = sb("esum", [P, NT], F32)
        esum2 = sb("esum2", [P, NT], F32)
        einv = sb("einv", [P, NT], F32)
        eT = sb("eT", [P, 2, NT, N], F16)

        early_rows = ax[3][:].rearrange("p w c n -> p (w c n)").bitcast(F32)
        b_row = early_rows[:, 0:2 * D].rearrange("p (l d) -> p l d", l=2)
        wab_row = early_rows[:, 2 * D:4 * D]
        wab = wab_row.rearrange("p (a c q) -> p a c q", a=2, c=NC)
        a_and_w = t_[3][:].rearrange("p w c n -> p (w c n)").bitcast(F32).rearrange("p (r d) -> p r d", d=D)
        ab = a_and_w[:, 0:2, :]
        wg = a_and_w[:, 2:4, :]
        stage_w = pT[:].rearrange("p a g k q -> p (a g k q)")[:, 0:NW * NC * D].rearrange(
            "p (w c d) -> p w c d", w=NW, c=NC)
        stage_adj = zm[:].bitcast(I32)
        stage_adjT = eT[:].rearrange("p w t n -> p (w t n)").bitcast(I32).rearrange("p (t n) -> p t n", t=NT)
        edge = aT[:]

        s_ps = [ctx.enter_context(nc.psum_tensor(f"s_ps{i}", [P, N], F32)) for i in range(2)]
        pt_ps = [ctx.enter_context(nc.psum_tensor(f"pt_ps{i}", [P, N], F32)) for i in range(2)]
        o_ps = ctx.enter_context(nc.psum_tensor("o_ps", [P, N], F32))
        side_ps = [ctx.enter_context(nc.psum_tensor(f"side_ps{i}", [P, N], F32)) for i in range(SIDE_BANKS)]

        setup_pool = sem("setup_pool")
        setup_act = sem("setup_act")
        setup_dve = sem("setup_dve")
        wab_ready, w_ready, b_ready, bo_ready = sem("wab_ready"), sem("w_ready"), sem("b_ready"), sem("bo_ready")
        qk_w_loaded, w_loaded, adj_loaded, row_loaded, b_qkv_loaded = (
            sem("qk_w_loaded"), sem("w_loaded"), sem("adj_loaded"), sem("row_loaded"), sem("b_qkv_loaded"))
        empty_step, power0_ready = sem("empty_step"), sem("power0_ready")
        b_col_ready, mask_ready = sem("b_col_ready"), sem("mask_ready")
        xt_loaded, xr_loaded, stored = sem("xt_loaded"), sem("xr_loaded"), sem("stored")
        xt_scaled, xt_hi, xt_lo, xr_scaled = sem("xt_scaled"), sem("xt_hi"), sem("xt_lo"), sem("xr_scaled")
        qk_done, qk_ready, qk_hi, qk_lo = sem("qk_done"), sem("qk_ready"), sem("qk_hi"), sem("qk_lo")
        xr_shifted = sem("xr_shifted")
        packed = [sem(f"packed{h}") for h in range(H)]
        v_done, v_ready = sem("v_done"), sem("v_ready")
        s_done, z_ready, p_ready, pt_done, pt_ready = (
            sem("s_done"), sem("z_ready"), sem("p_ready"), sem("pt_done"), sem("pt_ready"))
        rsum_ready = sem("rsum_ready")
        pv_done, rinv_ready, r_done, r_ready, o_ready, o_hi, o_lo = (
            sem("pv_done"), sem("rinv_ready"), sem("r_done"), sem("r_ready"), sem("o_ready"), sem("o_hi"),
            sem("o_lo"))
        y0_done, y0_ready = sem("y0_done"), sem("y0_ready")
        st_ready = [sem(f"st_ready{L}") for L in LAYERS]
        mv_ready = [sem(f"mv_ready{L}") for L in LAYERS]
        ve_ready = [sem(f"ve_ready{L}") for L in LAYERS]
        rstd_ready = [sem(f"rstd_ready{L}") for L in LAYERS]
        ln_ready = [sem(f"ln_ready{L}") for L in LAYERS]
        two = lambda name: {L: sem(f"{name}{L}") for L in (1, 3)}
        bias_added = two("bias_added")
        x_hi, x_lo = two("x_hi"), two("x_lo")
        ax_done, ax_hi, ax_lo = two("ax_done"), two("ax_hi"), two("ax_lo")
        mi_done, mi_ready, mj_done, mj_ready = two("mi_done"), two("mi_ready"), two("mj_done"), two("mj_ready")
        xT_done, xT_hi, xT_lo = ({L: sem(f"{name}{L}") for L in (1, 2, 3)} for name in ("xT_done", "xT_hi", "xT_lo"))
        db_done, zm_ready, s_col_done, scol_ready, wh_done, wh_hi, wh_lo = (
            sem("db_done"), sem("zm_ready"), sem("s_col_done"), sem("scol_ready"), sem("wh_done"), sem("wh_hi"),
            sem("wh_lo"))
        m_step, nm2_ready, zs_ready, lz_ready, e_ready, einv_step, einv_ready = (
            sem("m_step"), sem("nm2_ready"), sem("zs_ready"), sem("lz_ready"), sem("e_ready"), sem("einv_step"),
            sem("einv_ready"))
        ta_done, eT_hi, eT_lo, yo_done, y2_ready = (
            sem("ta_done"), sem("eT_hi"), sem("eT_lo"), sem("yo_done"), sem("y2_ready"))

        def count(per, b, k=0):
            value = per * b + k
            return max(0, value) if isinstance(value, int) else value

        def early(eng, value):
            if not isinstance(value, int):
                eng.compute_val(value)
            return value

        bank_read = {
            "q": (qk_ready, 4, lambda k: 2 * k + 1), "k": (qk_ready, 4, lambda k: 2 * k + 2),
            "v": (v_ready, 2, lambda k: k + 1), "r": (r_ready, 2, lambda k: k + 1),
            "y0": (y0_ready, 2, lambda k: k + 1),
            "db": (zm_ready, NT, lambda k: NT), "s": (scol_ready, 1, lambda k: 1),
            "wh": (wh_lo, 2, lambda k: k + 1), "ta": (eT_lo, NT, lambda k: k + 1),
            "yo": (y2_ready, NT, lambda k: 2 * k + 2),
        }
        for L in (1, 3):
            bank_read[f"ax{L}"] = (ax_lo[L], 2, lambda k: k + 1)
            bank_read[f"mi{L}"] = (mi_ready[L], NT, lambda k: 2 * k + 2)
            bank_read[f"mj{L}"] = (mj_ready[L], 2, lambda k: k + 1)

        for L in (1, 2, 3):
            bank_read[f"t{L}"] = (xT_lo[L], 2, lambda k: k + 1)
        xT_used = {1: mi_done[1], 2: wh_done, 3: mi_done[3]}

        def side_bank(name, part):
            return side_ps[PLACE[name, part] % SIDE_BANKS]

        def bank_free(name, part, b):
            me = PLACE[name, part]
            step, place = b + SLOT_OF[name, part] // SLOTS, me
            for _ in range(3 * len(SIDE)):
                place -= SIDE_BANKS
                if place < 0:
                    step, place = step - 1, place + len(SIDE) // SIDE_BANKS * SIDE_BANKS + (
                        SIDE_BANKS if me % SIDE_BANKS < len(SIDE) % SIDE_BANKS else 0)
                n, k, slot = SIDE_ORDER[place]
                if alive(step - slot // SLOTS):
                    s, per, read = bank_read[n]
                    return s, count(per, step - slot // SLOTS, read(k))
            return setup_act, 0

        def alive(b):
            return not isinstance(b, int) or 0 <= b < B

        def run_steps(eng, step):
            for j in range(LAST + 1):
                step(j)
            with eng.Fori(LAST + 1, B) as j:
                step(j)
            for j in range(B, B + LAST + 1):
                step(j)

        def unit(u):
            grp, r = divmod(u, GROUP)
            return 2 * (grp % 2) + r % 2, r // 2, grp // 2, grp % 2

        def sum_column(u):
            t, g, c, _ = unit(u)
            return (c * NT + t) * 4 + g

        def due(j, slot, slots):
            return [(part, j - s // SLOTS) for part, s in enumerate(slots)
                    if s % SLOTS == slot and alive(j - s // SLOTS)]

        block = ctx.enter_context(nc.Block())

        @block.sync
        def _(sp):
            order = {n: i for i, n in enumerate(names)}
            for n in ("q", "k", "v", "o", "1i", "1j", "2", "3i", "3j"):
                sp.dma_start(stage_w[:, order[n]],
                             wts[order[n]].rearrange("(c p) o -> p c o", p=P)).then_inc(qk_w_loaded if n in "qk" else w_loaded, 16)
                if n == "k":
                    sp.dma_start(xt[:], xT[0].rearrange("(c p) n -> p c n", p=P)).then_inc(xt_loaded, 16)
                    sp.dma_start(b_col[:], b_col_in).then_inc(b_qkv_loaded, 16)
            sp.dma_start(stage_adj, adj.rearrange("(t p) j -> p t j", p=P)).then_inc(adj_loaded, 16)
            sp.dma_start(stage_adjT, adjT.rearrange("(t p) j -> p t j", p=P)).then_inc(adj_loaded, 16)
            sp.dma_start(wg, w_gat.rearrange("(c p) o -> p c o", p=P)).then_inc(row_loaded, 16)
            for to, row in ((ab[:, 0, :], a_src), (ab[:, 1, :], a_dst), (bo_row[:], b_out),
                            (b_row[:, 0, :], b_layer[0]), (b_row[:, 1, :], b_layer[1])):
                sp.dma_start(to, row.unsqueeze(0).broadcast_to([P, D])).then_inc(row_loaded, 16)

            def load_xt(b):
                if isinstance(b, int) and b == 0:
                    return
                sp.wait_ge(xt_hi, count(1, b))
                sp.wait_ge(xt_lo, count(1, b))
                sp.dma_start(xt[:], xT[b].rearrange("(c p) n -> p c n", p=P)).then_inc(xt_loaded, 16)

            def load_xr(b):
                sp.wait_ge(y0_ready, count(2, b))
                sp.dma_start(xr[:], x[b].rearrange("(t p) d -> p t d", p=P)).then_inc(xr_loaded, 16)

            def pack(b, c):
                split = early(sp, count(4, b, 2 * c + 2))
                scored = early(sp, count(UNITS, b - 1, UNITS // 2 * (c + 1)))
                sp.wait_ge(setup_pool, 1)
                sp.wait_ge(qk_hi, split)
                sp.wait_ge(qk_lo, split)
                sp.wait_ge(s_done, scored)
                blocks = (slice(1, 3), slice(0, 3, 2), slice(1, 4, 2))
                for g in range(4):
                    for r in range(3):
                        sp.dma_start(qkp[DH * r:DH * r + DH, :, 4 * c + g, :],
                                     qk16[DH * g:DH * g + DH, c, blocks[r], :]).then_inc(packed[4 * c + g], 16)

            def store(b):
                sp.wait_ge(ln_ready[3], count(NT, b + 1))
                sp.dma_start(out[b].rearrange("(t p) d -> p t d", p=P), res[3][:]).then_inc(stored, 16)

            def step(j):
                at = WHEN["sync"]
                for slot in range(SLOTS):
                    for _, b in due(j, slot, at["load_xt"]):
                        load_xt(b)
                    for c, b in due(j, slot, at["pack"]):
                        pack(b, c)
                    for _, b in due(j, slot, at["load_xr"]):
                        load_xr(b)
                    for _, b in due(j, slot, at["store"]):
                        store(b)

            run_steps(sp, step)
            sp.wait_ge(stored, 16 * B)

        @block.gpsimd
        def _(pool):
            pool.memset(ident[:], 0.0).then_inc(setup_pool, 1)
            pool.memset(half_neg[:], -0.5).then_inc(setup_pool, 1)
            pool.wait_ge(setup_pool, 2)
            pool.affine_select(out=ident[:], in_=ident[:], compare_op=ALU.not_equal, fill=1.0, base=0,
                               pattern=[[-1, P]], channel_multiplier=1).then_inc(setup_pool, 1)

            def scale_xt(b):
                loaded = early(pool, count(16, b + 1))
                pool.wait_ge(setup_pool, 1)
                pool.wait_ge(xt_loaded, loaded)
                pool.tensor_scalar(xt[:], xt[:], XS, 1.0, ALU.mult, ALU.mult).then_inc(xt_scaled, 1)

            def split_xt(b):
                pool.wait_ge(xt_hi, count(1, b + 1))
                pool.wait_ge(v_done, count(2, b))
                pool.tensor_tensor(xt_l[:], xt[:], xt_h[:], ALU.subtract).then_inc(xt_lo, 1)

            def scale_xr(b):
                loaded = early(pool, count(16, b + 1))
                pool.wait_ge(setup_pool, 1)
                pool.wait_ge(xr_loaded, loaded)
                pool.tensor_scalar(xr[:], xr[:], XS, 1.0, ALU.mult, ALU.mult).then_inc(xr_scaled, 1)

            def shift_xr(b):
                pool.wait_ge(xr_scaled, count(1, b + 1))
                pool.wait_ge(bo_ready, 1)
                pool.tensor_tensor(xr[:], xr[:], bo_row[:].unsqueeze(1).broadcast_to([P, NT, D]),
                                   ALU.add).then_inc(xr_shifted, 1)

            def split_qk(b, n):
                pool.wait_ge(qk_hi, count(4, b, n + 1))
                w, c = "qk"[n % 2], n // 2
                pool.tensor_tensor(qk16[:, c, LOW[w], :], qk[:, n % 2, :], qk16[:, c, HIGH[w], :],
                                   ALU.subtract).then_inc(qk_lo, 1)

            def add_bias(b, L):
                pool.wait_ge(x_lo[L], count(1, b + 1))
                pool.wait_ge(xT_done[L], count(NC, b + 1))
                pool.wait_ge(b_ready, 2)
                pool.tensor_tensor(res[L][:], res[L][:], deg_b[L][:], ALU.add).then_inc(bias_added[L], 1)

            def split_x(b, L):
                pool.wait_ge(x_hi[L], count(1, b + 1))
                pool.wait_ge(ax_done[L], count(NC, b))
                pool.tensor_tensor(l_[L][:], res[L][:], h_[L][:], ALU.subtract).then_inc(x_lo[L], 1)

            def rsqrt(b, L):
                c1, c2 = (1.0 / (XS * XS), EPS) if L < 3 else (1.0, EPS * XS * XS)
                variances = early(pool, count(NT, b + 1))
                pool.wait_ge(setup_pool, 1)
                pool.wait_ge(mv_ready[L], variances)
                pool.tensor_scalar(ve[:, L, :], mv[:, L, :, 1], c1, c2, ALU.mult, ALU.add).then_inc(ve_ready[L], 1)
                pool.wait_ge(ve_ready[L], count(1, b + 1))
                if L == 0:
                    pool.wait_ge(power0_ready, 1)
                pool.tensor_tensor(rstd[:, L, :], ve[:, L, :], (half_neg if L else power0)[:], ALU.pow).then_inc(rstd_ready[L], 1)

            def step(j):
                at = WHEN["gpsimd"]
                for slot in range(SLOTS):
                    for L, b in due(j, slot, at["rsqrt"]):
                        rsqrt(b, L)
                    for n, b in due(j, slot, at["split_qk"]):
                        split_qk(b, n)
                    for _, b in due(j, slot, at["split_x3"]):
                        split_x(b, 3)
                    for _, b in due(j, slot, at["add_bias3"]):
                        add_bias(b, 3)
                    for _, b in due(j, slot, at["split_x1"]):
                        split_x(b, 1)
                    for _, b in due(j, slot, at["add_bias1"]):
                        add_bias(b, 1)
                    for _, b in due(j, slot, at["scale_xt"]):
                        scale_xt(b)
                    for _, b in due(j, slot, at["split_xt"]):
                        split_xt(b)
                    for _, b in due(j, slot, at["shift_xr"]):
                        scale_xr(b)
                        shift_xr(b)

            run_steps(pool, step)

        @block.scalar
        def _(act):
            act.wait_ge(qk_w_loaded, 32)
            act.activation(w_hi[:, 0:2], stage_w[:, 0:2], ACT.Copy, scale=WS).then_inc(setup_act, 1)

            def exp_scores(b, u):
                act.wait_ge(z_ready, count(UNITS, b, u + 1))
                act.wait_ge(pt_done, count(UNITS, b, u - RING + 1))
                if u % (UNITS // 2) == 0:
                    act.wait_ge(rinv_ready, count(2, b - 1, u // 16 + 1))
                act.activation(p[:, u % RING, :], z[:, u % RING, :], ACT.Exp, bias=nmax[:, u:u + 1], scale=-1.0,
                               accum_out=sum_p[:, sum_column(u):sum_column(u) + 1]).then_inc(p_ready, 1)

            def evict_pt(b, u):
                t, g, _, _ = unit(u)
                grp = u // GROUP
                act.wait_ge(pt_done, count(UNITS, b, u + 1))
                if u % GROUP == 0:
                    act.wait_ge(pv_done, count(4, b, grp - 1))
                act.activation(pT[:, grp % 2, g, :, P * (t % 2):P * (t % 2) + P],
                               pt_ps[u % 2][:].rearrange("p (k q) -> p k q", k=NT), ACT.Copy).then_inc(pt_ready, 1)

            def xt_high(b):
                act.wait_ge(xt_scaled, count(1, b + 1))
                act.wait_ge(v_done, count(2, b))
                act.activation(xt_h[:], xt[:], ACT.Copy).then_inc(xt_hi, 1)

            def qk_high(b, n):
                act.wait_ge(qk_ready, count(4, b, n + 1))
                if n % 2 == 0:
                    for g in range(4):
                        act.wait_ge(packed[4 * (n // 2) + g], count(48, b))
                act.activation(qk16[:, n // 2, HIGH["qk"[n % 2]], :], qk[:, n % 2, :], ACT.Copy).then_inc(qk_hi, 1)

            def v_evict(b, i):
                act.wait_ge(v_done, count(2, b, i + 1))
                act.wait_ge(pv_done, count(4, b))
                act.activation(v[:, 2 * i:2 * i + 2, :].rearrange("p t d -> p (t d)"), side_bank("v", i)[:],
                               ACT.Copy, scale=1.0 / (XS * WS)).then_inc(v_ready, 1)

            def r_evict(b, c):
                act.wait_ge(r_done, count(NC, b, c + 1))
                act.wait_ge(o_lo, count(NC, b, c))
                act.activation(o16[:], side_bank("r", c)[:], ACT.Copy, scale=XS).then_inc(r_ready, 1)

            def o_high(b, c):
                act.wait_ge(o_ready, count(NC, b, c + 1))
                act.wait_ge(y0_done, count(2, b))
                act.wait_ge(b_col_ready, 1)
                act.activation(o_h[:, c, :], o16[:], ACT.Identity, bias=b_col[:, 2, c:c + 1],
                               scale=1.0).then_inc(o_hi, 1)

            def x_high(b, L):
                act.wait_ge(ln_ready[L - 1], count(NT, b + 1))
                act.wait_ge(ax_done[L], count(NC, b))
                act.activation(h_[L][:], res[L][:], ACT.Copy).then_inc(x_hi[L], 1)

            def ax_high(b, L, c):
                act.wait_ge(ax_done[L], count(NC, b, c + 1))
                act.wait_ge(mj_done[L], count(2, b))
                act.activation(ax[L][:, 0, c, :], side_bank(f"ax{L}", c)[:], ACT.Copy,
                               scale=AXS / XS).then_inc(ax_hi[L], 1)

            def xT_high(b, L, c):
                act.wait_ge(xT_done[L], count(NC, b, c + 1))
                act.wait_ge(xT_used[L], count(2, b))
                act.activation(t_[L][:, 0, c, :], side_bank(f"t{L}", c)[:], ACT.Copy).then_inc(xT_hi[L], 1)

            def wh_high(b, i):
                act.wait_ge(wh_done, count(2, b, i + 1))
                act.wait_ge(yo_done, count(2, b))
                act.activation(wh[:, 0, 2 * i:2 * i + 2, :].rearrange("p t d -> p (t d)"), side_bank("wh", i)[:],
                               ACT.Copy, scale=1.0 / WS).then_inc(wh_hi, 1)

            def exp_gat(b, t):
                act.wait_ge(lz_ready, count(NT, b, t + 1))
                act.wait_ge(nm2_ready, count(1, b + 1))
                act.wait_ge(ta_done, count(NT, b, t - 1))
                act.wait_ge(einv_ready, count(1, b))
                act.activation(e[:, t % 2, :], zm[:, t, :], ACT.Exp, bias=nm2[:, t:t + 1], scale=1.0,
                               accum_out=esum[:, t:t + 1]).then_inc(e_ready, 1)

            def eT_high(b, t):
                act.wait_ge(ta_done, count(NT, b, t + 1))
                act.wait_ge(yo_done, count(2, b))
                act.activation(eT[:, 0, :, P * t:P * t + P],
                               side_bank("ta", t)[:].rearrange("p (k q) -> p k q", k=NT),
                               ACT.Copy, scale=ES).then_inc(eT_hi, 1)

            def step(j):
                at = WHEN["scalar"]
                for slot in range(SLOTS):
                    for u, b in due(j, slot, at["exp_scores"]):
                        exp_scores(b, u)
                    for u, b in due(j, slot, at["evict_pt"]):
                        evict_pt(b, u)
                    for c, b in due(j, slot, at["xT_high3"]):
                        xT_high(b, 3, c)
                    for _, b in due(j, slot, at["x_high3"]):
                        x_high(b, 3)
                    for c, b in due(j, slot, at["ax_high3"]):
                        ax_high(b, 3, c)
                    for t, b in due(j, slot, at["eT_high"]):
                        eT_high(b, t)
                    for t, b in due(j, slot, at["exp_gat"]):
                        exp_gat(b, t)
                    for i, b in due(j, slot, at["wh_high"]):
                        wh_high(b, i)
                    for c, b in due(j, slot, at["xT_high2"]):
                        xT_high(b, 2, c)
                    for c, b in due(j, slot, at["ax_high1"]):
                        ax_high(b, 1, c)
                    for c, b in due(j, slot, at["xT_high1"]):
                        xT_high(b, 1, c)
                    for _, b in due(j, slot, at["x_high1"]):
                        x_high(b, 1)
                    for c, b in due(j, slot, at["r_evict"]):
                        r_evict(b, c)
                    for c, b in due(j, slot, at["o_high"]):
                        o_high(b, c)
                    for i, b in due(j, slot, at["v_evict"]):
                        v_evict(b, i)
                    for _, b in due(j, slot, at["xt_high"]):
                        xt_high(b)
                    for n, b in due(j, slot, at["qk_high"]):
                        qk_high(b, n)
                if isinstance(j, int) and j == 0:
                    act.wait_ge(w_loaded, 16 * (NW - 2))
                    act.activation(w_hi[:, 2:NW], stage_w[:, 2:NW], ACT.Copy, scale=WS).then_inc(setup_act, 1)
                if isinstance(j, int) and j == 1:
                    act.wait_ge(wab_ready, 1)
                    act.activation(wab_h[:], wab, ACT.Copy, scale=WS).then_inc(setup_act, 1)

            run_steps(act, step)

        @block.vector
        def _(dve):
            dve.wait_ge(b_qkv_loaded, 16)
            dve.tensor_scalar(b_col[:], b_col[:], XS, None, ALU.mult).then_inc(b_col_ready, 1)
            dve.wait_ge(setup_act, 1)
            dve.scalar_tensor_tensor(w_lo[:, 0:2].rearrange("p w c d -> p (w c d)"),
                                     stage_w[:, 0:2].rearrange("p w c d -> p (w c d)"), WS,
                                     w_hi[:, 0:2].rearrange("p w c d -> p (w c d)"),
                                     ALU.mult, ALU.subtract).then_inc(w_ready, 1)

            def setup_before_attention():
                dve.wait_ge(adj_loaded, 32)
                dve.tensor_scalar(mask[:], stage_adj, 0.0, FAR, ALU.is_equal, ALU.mult).then_inc(mask_ready, 1)
                dve.wait_ge(mask_ready, 1)

            def setup_later(part):
                if part in (0, 1):
                    first, last = ((2, 4), (4, NW))[part]
                    dve.wait_ge(setup_act, 2)
                    dve.scalar_tensor_tensor(w_lo[:, first:last].rearrange("p w c d -> p (w c d)"),
                                             stage_w[:, first:last].rearrange("p w c d -> p (w c d)"), WS,
                                             w_hi[:, first:last].rearrange("p w c d -> p (w c d)"),
                                             ALU.mult, ALU.subtract).then_inc(w_ready, 1)
                elif part == 2:
                    dve.wait_ge(row_loaded, 16 * 6)
                    dve.tensor_scalar(bo_row[:], bo_row[:], XS, None, ALU.mult).then_inc(bo_ready, 1)
                    dve.tensor_scalar(edge, stage_adj, 0.0, None, ALU.not_equal).then_inc(setup_dve, 1)
                    dve.tensor_reduce(deg[:], stage_adj, AX.X, ALU.add).then_inc(setup_dve, 1)
                elif part == 3:
                    dve.wait_ge(setup_dve, 2)
                    dve.tensor_scalar(deg_s[:], deg[:], 1.0 / WS, None, ALU.mult).then_inc(setup_dve, 1)
                    dve.tensor_reduce(edges[:, 0, :], edge, AX.X, ALU.add).then_inc(empty_step, 1)
                    dve.wait_ge(empty_step, 1)
                    dve.reciprocal(edges[:, 1, :], edges[:, 0, :]).then_inc(empty_step, 1)
                    dve.wait_ge(empty_step, 2)
                    dve.tensor_scalar(power0[:], edges[:, 1, :], 0.0, -0.5, ALU.mult, ALU.add).then_inc(power0_ready, 1)
                elif part == 4:
                    dve.wait_ge(empty_step, 1)
                    dve.tensor_copy(aT[:], stage_adjT).then_inc(setup_dve, 1)
                elif part == 5:
                    for i in range(2):
                        for c in range(NC):
                            dve.tensor_tensor_reduce(zs[:, 0, 0:D], wg[:, c, :], ab[:, i, :], 1.0, 0.0,
                                                     ALU.mult, ALU.add, wa[:, i, c:c + 1]).then_inc(setup_dve, 1)
                            dve.wait_ge(setup_dve, 5 + 2 * i + c)
                elif part == 6:
                    dve.wait_ge(setup_pool, 3)
                    for i in range(2):
                        for c in range(NC):
                            last = dve.tensor_scalar(wab[:, i, c, :], ident[:], 0.0, wa[:, i, c:c + 1],
                                                     ALU.mult, ALU.add)
                    last.then_inc(wab_ready, 1)
                elif part in (7, 8):
                    i, L = ((0, 1), (1, 3))[part - 7]
                    for t in range(NT):
                        last = dve.tensor_scalar(deg_b[L][:, t, :], b_row[:, i, :], deg[:, t:t + 1], XS,
                                                 ALU.mult, ALU.mult)
                    last.then_inc(b_ready, 1)

            def setup_wab_low():
                dve.wait_ge(setup_act, 3)
                dve.scalar_tensor_tensor(wab_l[:].rearrange("p a c q -> p (a c q)"), wab_row, WS,
                                         wab_h[:].rearrange("p a c q -> p (a c q)"),
                                         ALU.mult, ALU.subtract).then_inc(setup_dve, 1)

            def row_max(b, u):
                t = unit(u)[0]
                scored, freed = early(dve, count(UNITS, b, u + 1)), early(dve, count(UNITS, b, u - RING + 1))
                dve.wait_ge(setup_pool, 1)
                dve.wait_ge(s_done, scored)
                dve.wait_ge(p_ready, freed)
                dve.tensor_tensor_reduce(z[:, u % RING, :], s_ps[u % 2][:], mask[:, t, :], -SCORE, -FAR,
                                         ALU.add, ALU.min, nmax[:, u:u + 1]).then_inc(z_ready, 1)

            def evict_qk(b, n):
                dve.wait_ge(qk_done, count(4, b, n + 1))
                dve.wait_ge(qk_hi, count(4, b, n - 1))
                dve.wait_ge(qk_lo, count(4, b, n - 1))
                dve.tensor_scalar(qk[:, n % 2, :], side_bank("qk"[n % 2], n // 2)[:], 1.0 / WS,
                                  b_col[:, n % 2, n // 2:n // 2 + 1], ALU.mult, ALU.add).then_inc(qk_ready, 1)

            def sum_inverse(b, c):
                dve.wait_ge(p_ready, count(UNITS, b, UNITS // 2 * (c + 1)))
                dve.reciprocal(rsum[:, c, :], sum_p[:, 16 * c:16 * c + 16]).then_inc(rsum_ready, 1)
                dve.wait_ge(rsum_ready, count(NC, b, c + 1))
                dve.wait_ge(r_done, count(NC, b, c))
                dve.tensor_copy(rinv[:].rearrange("p t g d -> p (t g) d"),
                                rsum[:, c, :].unsqueeze(2).broadcast_to([P, 16, DH])).then_inc(rinv_ready, 1)

            def normalise(b, c):
                dve.wait_ge(r_ready, count(NC, b, c + 1))
                dve.wait_ge(pv_done, count(4, b, 2 * c + 2))
                dve.tensor_tensor(o16[:], o_ps[:], o16[:], ALU.mult).then_inc(o_ready, 1)

            def o_low(b, c):
                dve.wait_ge(o_hi, count(NC, b, c + 1))
                dve.wait_ge(y0_done, count(2, b))
                dve.scalar_tensor_tensor(o_l[:, c, :], o16[:], b_col[:, 2, c:c + 1], o_h[:, c, :],
                                         ALU.add, ALU.subtract).then_inc(o_lo, 1)

            def add_y0(b, i):
                dve.wait_ge(y0_done, count(2, b, i + 1))
                dve.wait_ge(xr_shifted, count(1, b + 1))
                if i == 0:
                    dve.wait_ge(x_hi[1], count(1, b))
                    dve.wait_ge(x_lo[1], count(1, b))
                dve.scalar_tensor_tensor(
                    res[1][:, 2 * i:2 * i + 2, :].rearrange("p t d -> p (t d)"), side_bank("y0", i)[:], 1.0 / WS,
                    xr[:, 2 * i:2 * i + 2, :].rearrange("p t d -> p (t d)"),
                    ALU.mult, ALU.add).then_inc(y0_ready, 1)

            def ln_stats(b, L, t, src):
                dve.bn_stats(stats[:, L, t, :], src[:, t, :]).then_inc(st_ready[L], 1)

            def ln_mean_var(b, L):
                for t in range(NT):
                    statistics = early(dve, count(NT, b, t + 1))
                    dve.wait_ge(setup_pool, 1)
                    dve.wait_ge(st_ready[L], statistics)
                    dve.bn_aggr(mv[:, L, t, :], stats[:, L, t, :]).then_inc(mv_ready[L], 1)

            def ln_apply(b, L, i, src, dst):
                dve.wait_ge(rstd_ready[L], count(1, b + 1))
                for t in (2 * i, 2 * i + 1):
                    dve.tensor_scalar(dst[:, t, :], src[:, t, :], mv[:, L, t, 0:1], rstd[:, L, t:t + 1],
                                      ALU.subtract, ALU.mult).then_inc(ln_ready[L], 1)

            def xT_low(b, L, c):
                dve.wait_ge(xT_hi[L], count(NC, b, c + 1))
                dve.tensor_tensor(t_[L][:, 1, c, :], side_bank(f"t{L}", c)[:], t_[L][:, 0, c, :],
                                  ALU.subtract).then_inc(xT_lo[L], 1)

            def ax_low(b, L, c):
                dve.wait_ge(ax_hi[L], count(NC, b, c + 1))
                dve.scalar_tensor_tensor(ax[L][:, 1, c, :], side_bank(f"ax{L}", c)[:], AXS / XS, ax[L][:, 0, c, :],
                                         ALU.mult, ALU.subtract).then_inc(ax_lo[L], 1)

            def add_mi(b, L, i):
                dve.wait_ge(mi_done[L], count(2, b, i + 1))
                dve.wait_ge(bias_added[L], count(1, b + 1))
                for t in (2 * i, 2 * i + 1):
                    dve.scalar_tensor_tensor(res[L][:, t, :], side_bank(f"mi{L}", i)[:, D * (t % 2):D * (t % 2) + D],
                                             deg_s[:, t:t + 1], res[L][:, t, :],
                                             ALU.mult, ALU.add).then_inc(mi_ready[L], 1)

            def add_mj(b, L, i):
                dve.wait_ge(mj_done[L], count(2, b, i + 1))
                dve.wait_ge(mi_ready[L], count(NT, b, 2 * i + 2))
                pair = res[L][:, 2 * i:2 * i + 2, :].rearrange("p t d -> p (t d)")
                dve.scalar_tensor_tensor(pair, side_bank(f"mj{L}", i)[:], XS / (AXS * WS), pair,
                                         ALU.mult, ALU.add).then_inc(mj_ready[L], 1)

            def stats_mj(b, L, i):
                dve.wait_ge(mj_ready[L], count(2, b, i + 1))
                for t in (2 * i, 2 * i + 1):
                    ln_stats(b, L, t, res[L])

            def neighbour_max(b, t):
                done, freed = early(dve, count(1, b + 1)), early(dve, count(NT, b))
                dve.wait_ge(setup_pool, 1)
                dve.wait_ge(db_done, done)
                dve.wait_ge(e_ready, freed)
                dve.tensor_tensor_reduce(zm[:, t, :], side_bank("db", 0)[:], mask[:, t, :], 1.0 / (XS * WS),
                                         FAR, ALU.add, ALU.max, dmax[:, t:t + 1]).then_inc(zm_ready, 1)

            def logit_max(b):
                dve.wait_ge(s_col_done, count(1, b + 1))
                dve.tensor_scalar(scol[:], side_bank("s", 0)[:, 0:NT], 1.0 / (XS * WS), None,
                                  ALU.mult).then_inc(scol_ready, 1)
                dve.wait_ge(scol_ready, count(1, b + 1))
                dve.wait_ge(zm_ready, count(NT, b + 1))
                dve.tensor_tensor(mcol[:, 0, :], dmax[:], scol[:], ALU.add).then_inc(m_step, 1)
                dve.wait_ge(m_step, count(2, b, 1))
                dve.scalar_tensor_tensor(mcol[:, 1, :], mcol[:, 0, :], SLOPE, mcol[:, 0, :],
                                         ALU.mult, ALU.max).then_inc(m_step, 1)
                dve.wait_ge(m_step, count(2, b, 2))
                dve.tensor_scalar(nm2[:], mcol[:, 1, :], -1.0e30, -1.0, ALU.max, ALU.mult).then_inc(nm2_ready, 1)

            def logits(b, t):
                dve.wait_ge(lz_ready, count(NT, b, t - 1))
                dve.tensor_scalar(zs[:, t % 2, :], zm[:, t, :], scol[:, t:t + 1], SLOPE,
                                  ALU.add, ALU.mult).then_inc(zs_ready, 1)
                dve.wait_ge(zs_ready, count(NT, b, t + 1))
                dve.scalar_tensor_tensor(zm[:, t, :], zm[:, t, :], scol[:, t:t + 1], zs[:, t % 2, :],
                                         ALU.add, ALU.max).then_inc(lz_ready, 1)

            def wh_low(b, i):
                dve.wait_ge(wh_hi, count(2, b, i + 1))
                dve.scalar_tensor_tensor(wh[:, 1, 2 * i:2 * i + 2, :].rearrange("p t d -> p (t d)"),
                                         side_bank("wh", i)[:], 1.0 / WS,
                                         wh[:, 0, 2 * i:2 * i + 2, :].rearrange("p t d -> p (t d)"),
                                         ALU.mult, ALU.subtract).then_inc(wh_lo, 1)

            def eT_low(b, t):
                dve.wait_ge(eT_hi, count(NT, b, t + 1))
                dve.scalar_tensor_tensor(eT[:, 1, :, P * t:P * t + P],
                                         side_bank("ta", t)[:].rearrange("p (k q) -> p k q", k=NT), ES,
                                         eT[:, 0, :, P * t:P * t + P], ALU.mult, ALU.subtract).then_inc(eT_lo, 1)

            def gat_inverse(b):
                dve.wait_ge(e_ready, count(NT, b + 1))
                dve.tensor_scalar(esum2[:], esum[:], 1.0e-30, ES, ALU.max, ALU.mult).then_inc(einv_step, 1)
                dve.wait_ge(einv_step, count(1, b + 1))
                dve.reciprocal(einv[:], esum2[:]).then_inc(einv_ready, 1)

            def add_yo(b, i):
                dve.wait_ge(yo_done, count(2, b, i + 1))
                dve.wait_ge(einv_ready, count(1, b + 1))
                for t in (2 * i, 2 * i + 1):
                    dve.scalar_tensor_tensor(res[2][:, t, :], side_bank("yo", i)[:, D * (t % 2):D * (t % 2) + D],
                                             einv[:, t:t + 1], res[2][:, t, :],
                                             ALU.mult, ALU.add).then_inc(y2_ready, 1)

            def stats_y0(b, i):
                dve.wait_ge(y0_ready, count(2, b, i + 1))
                for t in (2 * i, 2 * i + 1):
                    ln_stats(b, 0, t, res[1])

            def stats_yo(b, i):
                dve.wait_ge(y2_ready, count(NT, b, 2 * i + 2))
                for t in (2 * i, 2 * i + 1):
                    ln_stats(b, 2, t, res[2])

            def step(j):
                at = WHEN["vector"]
                for slot in range(SLOTS):
                    for u, b in due(j, slot, at["row_max"]):
                        row_max(b, u)
                    for c, b in due(j, slot, at["xT_low3"]):
                        xT_low(b, 3, c)
                    for c, b in due(j, slot, at["ax_low3"]):
                        ax_low(b, 3, c)
                    for i, b in due(j, slot, at["add_mi3"]):
                        add_mi(b, 3, i)
                    for i, b in due(j, slot, at["add_mj3"]):
                        add_mj(b, 3, i)
                        stats_mj(b, 3, i)
                    for _, b in due(j, slot, at["mean_var3"]):
                        ln_mean_var(b, 3)
                    for i, b in due(j, slot, at["apply3"]):
                        ln_apply(b, 3, i, res[3], res[3])
                    for i, b in due(j, slot, at["add_yo"]):
                        if i == 0:
                            gat_inverse(b)
                        add_yo(b, i)
                        stats_yo(b, i)
                    for t, b in due(j, slot, at["eT_low"]):
                        eT_low(b, t)
                    for i, b in due(j, slot, at["wh_low"]):
                        wh_low(b, i)
                    for _, b in due(j, slot, at["mean_var2"]):
                        ln_mean_var(b, 2)
                    for i, b in due(j, slot, at["apply2"]):
                        dve.wait_ge(stored, count(16, b))
                        ln_apply(b, 2, i, res[2], res[3])
                    for c, b in due(j, slot, at["xT_low2"]):
                        xT_low(b, 2, c)
                    for t, b in due(j, slot, at["neighbour_max"]):
                        neighbour_max(b, t)
                    for _, b in due(j, slot, at["logit_max"]):
                        logit_max(b)
                    for t, b in due(j, slot, at["logits"]):
                        logits(b, t)
                    for c, b in due(j, slot, at["xT_low1"]):
                        xT_low(b, 1, c)
                    for c, b in due(j, slot, at["ax_low1"]):
                        ax_low(b, 1, c)
                    for i, b in due(j, slot, at["add_mi1"]):
                        add_mi(b, 1, i)
                    for i, b in due(j, slot, at["add_mj1"]):
                        add_mj(b, 1, i)
                        stats_mj(b, 1, i)
                    for _, b in due(j, slot, at["mean_var1"]):
                        ln_mean_var(b, 1)
                    for i, b in due(j, slot, at["apply1"]):
                        ln_apply(b, 1, i, res[1], res[2])
                    for c, b in due(j, slot, at["sum_inverse"]):
                        sum_inverse(b, c)
                    for c, b in due(j, slot, at["normalise"]):
                        normalise(b, c)
                    for c, b in due(j, slot, at["o_low"]):
                        o_low(b, c)
                    for i, b in due(j, slot, at["add_y0"]):
                        add_y0(b, i)
                        stats_y0(b, i)
                    for _, b in due(j, slot, at["mean_var0"]):
                        ln_mean_var(b, 0)
                    for i, b in due(j, slot, at["apply0"]):
                        ln_apply(b, 0, i, res[1], res[1])
                    for n, b in due(j, slot, at["evict_qk"]):
                        evict_qk(b, n)
                    if isinstance(j, int) and j == 1 and slot in SETUP_SLOTS:
                        setup_later(SETUP_SLOTS.index(slot))
                if isinstance(j, int) and j == 0:
                    setup_before_attention()
                if isinstance(j, int) and j == 1:
                    setup_wab_low()

            run_steps(dve, step)

        @block.tensor
        def _(pe):
            pe.wait_ge(w_ready, 1)
            pe.wait_ge(setup_pool, 3)

            def scores(b, u):
                t, g, c, _ = unit(u)
                h = 4 * c + g
                if u % (UNITS // 2) in range(0, GROUP, 2):
                    pe.wait_ge(packed[h], count(48, b + 1))
                pe.wait_ge(z_ready, count(UNITS, b, u - 1))
                pe.matmul(s_ps[u % 2][:], qkp[:, 0, h, P * t:P * t + P], qkp[:, 1, h, :],
                          start=True, stop=True).then_inc(s_done, 1)

            def transpose_p(b, u):
                pe.wait_ge(p_ready, count(UNITS, b, u + 1))
                pe.wait_ge(pt_ready, count(UNITS, b, u - 1))
                for k in range(NT):
                    mm = pe.transpose(pt_ps[u % 2][:, P * k:P * k + P], p[:, u % RING, P * k:P * k + P], ident[:])
                mm.then_inc(pt_done, 1)

            def times_v(b, grp, part):
                c, th = divmod(grp, 2)
                if part == 0:
                    pe.wait_ge(pt_ready, count(UNITS, b, GROUP * (grp + 1)))
                    pe.wait_ge(v_ready, count(2, b + 1))
                    if th == 0:
                        pe.wait_ge(o_ready, count(NC, b, c))
                for k in (2 * part, 2 * part + 1):
                    for g in range(4):
                        h = 4 * c + g
                        mm = pe.matmul(o_ps[DH * g:DH * g + DH, HALF * th:HALF * th + HALF],
                                       v[:, k, DH * h:DH * h + DH], pT[:, grp % 2, g, k, :],
                                       start=(k == 0), stop=(k == NT - 1))
                if part == 1:
                    mm.then_inc(pv_done, 1)

            def product(dst, pairs):
                for n, (lhs, rhs) in enumerate(pairs):
                    mm = pe.matmul(dst, lhs, rhs, start=(n == 0), stop=(n == len(pairs) - 1))
                return mm

            def split_pairs(lhs_h, lhs_l, rhs_h, rhs_l):
                return [(lhs_h, rhs_h), (lhs_l, rhs_h), (lhs_h, rhs_l)]

            def project_T(dst, w, c, xh, xl):
                o = slice(P * c, P * c + P)
                pairs = [q for k in range(NC) for q in split_pairs(WH[w][:, k, o], WL[w][:, k, o],
                                                                   xh[:, k, :], xl[:, k, :])]
                return product(dst[:], pairs)

            def project(dst, w, i, xh, xl):
                for t in (2 * i, 2 * i + 1):
                    o = slice(P * t, P * t + P)
                    pairs = [q for k in range(NC) for q in split_pairs(xh[:, k, o], xl[:, k, o],
                                                                       WH[w][:, k, :], WL[w][:, k, :])]
                    mm = product(dst[:, D * (t % 2):D * (t % 2) + D], pairs)
                return mm

            def project_qk(b, n):
                pe.wait_ge(xt_hi, count(1, b + 1))
                pe.wait_ge(xt_lo, count(1, b + 1))
                w = "qk"[n % 2]
                pe.wait_ge(*bank_free(w, n // 2, b))
                bank = side_bank(w, n // 2)
                project_T(bank, w, n // 2, xt_h, xt_l).then_inc(qk_done, 1)

            def values(b, i):
                pe.wait_ge(w_ready, 2)
                pe.wait_ge(*bank_free("v", i, b))
                bank = side_bank("v", i)
                project(bank, "v", i, xt_h, xt_l).then_inc(v_done, 1)

            def spread_inverse(b, c):
                pe.wait_ge(rinv_ready, count(NC, b, c + 1))
                pe.wait_ge(*bank_free("r", c, b))
                bank = side_bank("r", c)
                for t in range(NT):
                    mm = pe.transpose(bank[:, P * t:P * t + P], rinv[:, t].rearrange("p g d -> p (g d)"), ident[:])
                mm.then_inc(r_done, 1)

            def output(b, i):
                pe.wait_ge(o_hi, count(NC, b + 1))
                pe.wait_ge(o_lo, count(NC, b + 1))
                pe.wait_ge(*bank_free("y0", i, b))
                bank = side_bank("y0", i)
                project(bank, "o", i, o_h, o_l).then_inc(y0_done, 1)

            def transpose_x(b, L, c):
                pe.wait_ge(ln_ready[L - 1], count(NT, b + 1))
                pe.wait_ge(*bank_free(f"t{L}", c, b))
                bank = side_bank(f"t{L}", c)
                for t in range(NT):
                    mm = pe.transpose(bank[:, P * t:P * t + P], res[L][:, t, P * c:P * c + P], ident[:])
                mm.then_inc(xT_done[L], 1)

            def aggregate(b, L, c):
                pe.wait_ge(x_hi[L], count(1, b + 1))
                pe.wait_ge(x_lo[L], count(1, b + 1))
                pe.wait_ge(*bank_free(f"ax{L}", c, b))
                bank = side_bank(f"ax{L}", c)
                pairs = [(s[L][:, t, P * c:P * c + P], aT[:, t, :]) for s in (h_, l_) for t in range(NT)]
                product(bank[:], pairs).then_inc(ax_done[L], 1)

            def own_term(b, L, i):
                pe.wait_ge(xT_lo[L], count(NC, b + 1))
                pe.wait_ge(*bank_free(f"mi{L}", i, b))
                bank = side_bank(f"mi{L}", i)
                project(bank, f"{L}i", i, t_[L][:, 0], t_[L][:, 1]).then_inc(mi_done[L], 1)

            def neighbour_term(b, L, i):
                pe.wait_ge(ax_lo[L], count(NC, b + 1))
                pe.wait_ge(*bank_free(f"mj{L}", i, b))
                bank = side_bank(f"mj{L}", i)
                project(bank, f"{L}j", i, ax[L][:, 0], ax[L][:, 1]).then_inc(mj_done[L], 1)

            def gat_dst(b):
                pe.wait_ge(xT_lo[2], count(NC, b + 1))
                pe.wait_ge(*bank_free("db", 0, b))
                bank = side_bank("db", 0)
                pairs = [q for k in range(NC) for q in split_pairs(wab_h[:, 1, k, :], wab_l[:, 1, k, :],
                                                                   t_[2][:, 0, k, :], t_[2][:, 1, k, :])]
                product(bank[:], pairs).then_inc(db_done, 1)

            def gat_src(b):
                pe.wait_ge(*bank_free("s", 0, b))
                bank = side_bank("s", 0)
                for t in range(NT):
                    o = slice(P * t, P * t + P)
                    pairs = [q for k in range(NC) for q in split_pairs(t_[2][:, 0, k, o], t_[2][:, 1, k, o],
                                                                       wab_h[:, 0, k, 0:1], wab_l[:, 0, k, 0:1])]
                    mm = product(bank[:, t:t + 1], pairs)
                mm.then_inc(s_col_done, 1)

            def gat_wh(b, i):
                pe.wait_ge(*bank_free("wh", i, b))
                bank = side_bank("wh", i)
                project(bank, "2", i, t_[2][:, 0], t_[2][:, 1]).then_inc(wh_done, 1)

            def transpose_e(b, t):
                pe.wait_ge(e_ready, count(NT, b, t + 1))
                pe.wait_ge(*bank_free("ta", t, b))
                bank = side_bank("ta", t)
                for k in range(NT):
                    mm = pe.transpose(bank[:, P * k:P * k + P], e[:, t % 2, P * k:P * k + P], ident[:])
                mm.then_inc(ta_done, 1)

            def gat_out(b, i, t):
                pe.wait_ge(eT_lo, count(NT, b, t + 1))
                if t % 2 == 0:
                    pe.wait_ge(wh_lo, count(2, b + 1))
                    pe.wait_ge(*bank_free("yo", i, b))
                bank = side_bank("yo", i)
                o = slice(P * t, P * t + P)
                pairs = [q for k in range(NT) for q in split_pairs(eT[:, 0, k, o], eT[:, 1, k, o],
                                                                   wh[:, 0, k, :], wh[:, 1, k, :])]
                mm = product(bank[:, D * (t % 2):D * (t % 2) + D], pairs)
                if t % 2 == 1:
                    mm.then_inc(yo_done, 1)

            def step(j):
                at = WHEN["tensor"]
                if isinstance(j, int) and j == 2:
                    pe.wait_ge(w_ready, 3)
                    pe.wait_ge(setup_dve, 9)
                for slot in range(SLOTS):
                    for u, b in due(j, slot, at["scores"]):
                        scores(b, u)
                    for u, b in due(j, slot, at["transpose_p"]):
                        transpose_p(b, u)
                    for part, b in due(j, slot, at["times_v"]):
                        times_v(b, part // 2, part % 2)
                    for name, part, s in SIDE_ORDER:
                        b = j - s // SLOTS
                        if s % SLOTS != slot or not alive(b):
                            continue
                        if name in ("q", "k"):
                            project_qk(b, 2 * part + "qk".index(name))
                        elif name == "v":
                            values(b, part)
                        elif name == "r":
                            spread_inverse(b, part)
                        elif name == "y0":
                            output(b, part)
                        elif name == "db":
                            gat_dst(b)
                        elif name == "s":
                            gat_src(b)
                        elif name == "wh":
                            gat_wh(b, part)
                        elif name == "ta":
                            transpose_e(b, part)
                        elif name == "yo":
                            gat_out(b, part, 2 * part)
                            gat_out(b, part, 2 * part + 1)
                        elif name[:-1] == "t":
                            transpose_x(b, int(name[-1]), part)
                        elif name[:-1] == "ax":
                            aggregate(b, int(name[-1]), part)
                        elif name[:-1] == "mi":
                            own_term(b, int(name[-1]), part)
                        elif name[:-1] == "mj":
                            neighbour_term(b, int(name[-1]), part)

            run_steps(pe, step)


def kernel(x, adj, L0_gnn_Wq, L0_gnn_bq, L0_gnn_Wk, L0_gnn_bk, L0_gnn_Wv, L0_gnn_bv, L0_gnn_Wo, L0_gnn_bo,
           L1_gnn_W, L1_gnn_b, L2_gnn_W, L2_gnn_a_src, L2_gnn_a_dst, L3_gnn_W, L3_gnn_b):
    import numpy as np
    import concourse.bacc as bacc
    from concourse.bass_utils import run_bass_kernel_spmd

    nc = bacc.Bacc("TRN2", target_bir_lowering=False, num_devices=1)
    arrays = {}

    def given(name, a):
        a = np.ascontiguousarray(a)
        arrays[name] = a
        return nc.dram_tensor(name, a.shape, mybir.dt.from_np(a.dtype), kind="ExternalInput").ap()

    D = x.shape[2]
    x, adj = np.asarray(x), np.asarray(adj)
    w1, w3 = np.asarray(L1_gnn_W), np.asarray(L3_gnn_W)
    weights = [("wq", np.asarray(L0_gnn_Wq).T), ("wk", np.asarray(L0_gnn_Wk).T), ("wv", np.asarray(L0_gnn_Wv).T),
               ("wo", np.asarray(L0_gnn_Wo).T), ("w1i", w1[:, :D].T), ("w1j", w1[:, D:].T),
               ("w2", np.asarray(L2_gnn_W)), ("w3i", w3[:, :D].T), ("w3j", w3[:, D:].T)]
    wts = [given(n, a) for n, a in weights]
    b_qkv = np.stack([np.asarray(b) for b in (L0_gnn_bq, L0_gnn_bk, L0_gnn_bv)]).reshape(3, D // P, P)
    b_layer = [given("b1", L1_gnn_b), given("b3", L3_gnn_b)]
    out = nc.dram_tensor("out", x.shape, F32, kind="ExternalOutput").ap()
    build(nc, given("x", x), given("xT", x.transpose(0, 2, 1)), given("adj", adj), given("adjT", adj.T), wts,
          wts[6], given("a_src", L2_gnn_a_src), given("a_dst", L2_gnn_a_dst), given("b_qkv", b_qkv.transpose(2, 0, 1)),
          given("bo", L0_gnn_bo), b_layer, out)
    r = run_bass_kernel_spmd(nc, [arrays], core_ids=[0])
    return r.results[0]["out"]
```
